# Optimizing a Trainium2 kernel written in Bass

```python
import numpy as np
import jax
import jax.numpy as jnp

def _softmax(x, axis=-1):
    return jax.nn.softmax(x, axis=axis)

def _gelu(x):
    return jax.nn.gelu(x, approximate=True)

def _silu(x):
    return jax.nn.silu(x)

def _sigmoid(x):
    return jax.nn.sigmoid(x)

def _layernorm(x, axis=-1, eps=1e-05):
    m = jnp.mean(x, axis=axis, keepdims=True)
    v = jnp.var(x, axis=axis, keepdims=True)
    return (x - m) / jnp.sqrt(v + eps)

def _scatter_add(tgt, idx, src, axis=0):
    return tgt.at[idx].add(src)

def _segment_sum(src, seg, n):
    return jax.ops.segment_sum(src, seg, n)
kernel_name = 'mk_seq_preln_d1_jaxref_r8_d914cf'

def setup_inputs(seed: int=0):
    np.random.seed(seed)
    _w = jnp.asarray

    def _L0_attn_setup():
        import jax, jax.numpy as jnp
        import numpy as np
        N_HEADS = 16
        HEAD_DIM = 64
        DIM = 128
        BATCH = 2
        SEQ = 256
        key = jax.random.key(seed)
        ks = jax.random.split(key, 6)
        hd = N_HEADS * HEAD_DIM
        scale_in = 1.0 / np.sqrt(DIM)
        scale_out = 1.0 / np.sqrt(hd)
        return {'x': jax.random.normal(ks[0], (BATCH, SEQ, DIM), dtype=jnp.float32), 'Wq': jax.random.normal(ks[1], (DIM, hd), dtype=jnp.float32) * scale_in, 'Wk': jax.random.normal(ks[2], (DIM, hd), dtype=jnp.float32) * scale_in, 'Wv': jax.random.normal(ks[3], (DIM, hd), dtype=jnp.float32) * scale_in, 'Wo': jax.random.normal(ks[4], (hd, DIM), dtype=jnp.float32) * scale_out, 'bo': jnp.zeros((DIM,), dtype=jnp.float32)}
    _L0_attn_in = _L0_attn_setup()

    def _L0_ffn_setup():
        import jax, jax.numpy as jnp
        import numpy as np
        NUM_EXPERTS = 160
        TOP_K = 8
        ROUTED_SCALE = 2.5
        HIDDEN = 128
        INTER = 64
        key = jax.random.key(seed)
        ks = jax.random.split(key, 7)
        B, S = (1, 256)
        return {'hidden_states': jax.random.normal(ks[0], (B, S, HIDDEN), dtype=jnp.float32), 'router_w': jax.random.normal(ks[1], (NUM_EXPERTS, HIDDEN), dtype=jnp.float32) * 0.02, 'expert_bias': jnp.zeros((NUM_EXPERTS,), dtype=jnp.float32), 'w_gate': jax.random.normal(ks[2], (NUM_EXPERTS, INTER, HIDDEN), dtype=jnp.float32) * 0.02, 'w_down': jax.random.normal(ks[3], (NUM_EXPERTS, HIDDEN, INTER), dtype=jnp.float32) * 0.02, 'w_gate_shared': jax.random.normal(ks[4], (INTER, HIDDEN), dtype=jnp.float32) * 0.02, 'w_down_shared': jax.random.normal(ks[5], (HIDDEN, INTER), dtype=jnp.float32) * 0.02}
    _L0_ffn_in = _L0_ffn_setup()
    _d = {'L0_attn_x': _L0_attn_in['x'], 'L0_attn_Wq': _L0_attn_in['Wq'], 'L0_attn_Wk': _L0_attn_in['Wk'], 'L0_attn_Wv': _L0_attn_in['Wv'], 'L0_attn_Wo': _L0_attn_in['Wo'], 'L0_attn_bo': _L0_attn_in['bo'], 'L0_ffn_router_w': _L0_ffn_in['router_w'], 'L0_ffn_expert_bias': _L0_ffn_in['expert_bias'], 'L0_ffn_w_gate': _L0_ffn_in['w_gate'], 'L0_ffn_w_down': _L0_ffn_in['w_down'], 'L0_ffn_w_gate_shared': _L0_ffn_in['w_gate_shared'], 'L0_ffn_w_down_shared': _L0_ffn_in['w_down_shared']}
    _x0 = _d['L0_attn_x']
    _d['L0_attn_x'] = jax.random.normal(jax.random.fold_in(jax.random.key(seed), 1), (16, 256, 128), dtype=_x0.dtype)
    del _x0
    return _d

def reference(L0_attn_x, L0_attn_Wq, L0_attn_Wk, L0_attn_Wv, L0_attn_Wo, L0_attn_bo, L0_ffn_router_w, L0_ffn_expert_bias, L0_ffn_w_gate, L0_ffn_w_down, L0_ffn_w_gate_shared, L0_ffn_w_down_shared):

    def _L0_attn_ref(x, Wq, Wk, Wv, Wo, bo):
        import jax, jax.numpy as jnp
        import numpy as np
        N_HEADS = 16
        HEAD_DIM = 64
        DIM = 128
        BATCH = 2
        SEQ = 256
        b, s, _ = x.shape
        q = (x @ Wq).reshape(b, s, N_HEADS, HEAD_DIM)
        k = (x @ Wk).reshape(b, s, N_HEADS, HEAD_DIM)
        v = (x @ Wv).reshape(b, s, N_HEADS, HEAD_DIM)
        dot = jnp.einsum('bihd,bkhd->bhik', q, k)
        w = jax.nn.softmax(dot / jnp.sqrt(jnp.float32(HEAD_DIM)), axis=-1)
        a = jnp.einsum('bhij,bjhd->bihd', w, v)
        a = a.reshape(b, s, N_HEADS * HEAD_DIM)
        return a @ Wo + bo

    def _L0_ffn_ref(hidden_states, router_w, expert_bias, w_gate, w_down, w_gate_shared, w_down_shared):
        import jax, jax.numpy as jnp
        import numpy as np
        NUM_EXPERTS = 160
        TOP_K = 8
        ROUTED_SCALE = 2.5
        HIDDEN = 128
        INTER = 64
        B, S, H = hidden_states.shape
        x = hidden_states.reshape(-1, H)
        T = x.shape[0]
        logits = x @ router_w.T + expert_bias[None, :]
        probs = jax.nn.sigmoid(logits)
        top_w, top_idx = jax.lax.top_k(probs, TOP_K)
        top_w = top_w / (jnp.sum(top_w, axis=-1, keepdims=True) + 1e-09)
        top_w = top_w * ROUTED_SCALE
        combine = jnp.zeros((T, NUM_EXPERTS), dtype=x.dtype)
        combine = combine.at[jnp.arange(T)[:, None], top_idx].set(top_w)
        h1 = jax.nn.silu(jnp.einsum('th,eih->eti', x, w_gate))
        h1w = h1 * combine.T[:, :, None]
        routed = jnp.einsum('eti,ehi->th', h1w, w_down)
        shared = jax.nn.silu(x @ w_gate_shared.T) @ w_down_shared.T
        return (routed + shared).reshape(B, S, H)
    x = L0_attn_x
    x = x + _L0_attn_ref(_layernorm(x, axis=-1), L0_attn_Wq, L0_attn_Wk, L0_attn_Wv, L0_attn_Wo, L0_attn_bo)
    x = x + _L0_ffn_ref(_layernorm(x, axis=-1), L0_ffn_router_w, L0_ffn_expert_bias, L0_ffn_w_gate, L0_ffn_w_down, L0_ffn_w_gate_shared, L0_ffn_w_down_shared)
    return x

_drawn_inputs = setup_inputs


def setup_inputs(seed=0):
    import zlib

    import numpy as np

    out = dict(_drawn_inputs(seed))
    spreads = {'L0_attn_bo': (0.0, 0.1), 'L0_ffn_expert_bias': (0.0, 0.578)}
    factors = {'L0_ffn_router_w': 3.685,
     'L0_ffn_w_gate': 3.522,
     'L0_ffn_w_down': 3.508,
     'L0_ffn_w_gate_shared': 3.117,
     'L0_ffn_w_down_shared': 3.07}
    for name, (base, spread) in spreads.items():
        noise = np.random.default_rng([zlib.crc32(name.encode()), seed]).standard_normal(out[name].shape)
        drawn = base * np.exp(spread * noise) if base else spread * noise
        out[name] = jnp.asarray(drawn.astype(out[name].dtype))
    for name, factor in factors.items():
        out[name] = (out[name] * factor).astype(out[name].dtype)
    return out
```

```python
import concourse.bass as bass
from concourse import mybir
from contextlib import ExitStack

F32 = mybir.dt.float32
F32R = mybir.dt.float32r
BF16 = mybir.dt.bfloat16
I32 = mybir.dt.int32
U32 = mybir.dt.uint32
ALU = mybir.AluOpType
ACT = mybir.ActivationFunctionType
AX = mybir.AxisListType

P = 128
B, SEQ, D = 16, 256, 128
H, DH = 16, 64
G = H // 2
T = B * SEQ
NT = T // P
TB = SEQ // P
E, INTER, TOPK = 160, 64, 8
ROUTED_SCALE = 2.5
EPS = 1e-5
NSTEP = B * G
NBLK = T * TOPK // P + E
GB = 4
RING = 4
NGRP = NBLK // GB
BC = -(-NBLK // P)
assert NGRP % RING == 0
SCAT = [0, 0, 3, 3, 3, 3, 2, 2]
assert sum(SCAT) == TB * TOPK


def build(nc, x, wq, wk, wv, wo, bo, rwT, ebias, wgT, wdT, wgsT, wdsT, out):
    slot_x = nc.dram_tensor("slot_x", [NBLK * P, D], F32).ap()
    block_y = nc.dram_tensor("block_y", [NBLK * P, D], F32).ap()

    with ExitStack() as ctx:
        def sb(name, shape, dt=F32, at=ctx):
            return at.enter_context(nc.sbuf_tensor(name, shape, dt))

        def sem(name):
            return ctx.enter_context(nc.semaphore(name))

        def wait(eng, s, value):
            if not isinstance(value, int) or value > 0:
                eng.wait_ge(s, value)

        held = {}

        def wait_apart(eng, s, value):
            if isinstance(value, int):
                wait(eng, s, value)
            else:
                eng.reg_mov(held[eng], value)
                eng.wait_ge(consts, 5)
                eng.wait_ge(s, held[eng])

        x_res = sb("x_res", [P, NT + TB, D])
        xn2T_res = sb("xn2T_res", [P, T])
        wE_res = sb("wE_res", [P, NT, TOPK])
        pos_u = sb("pos_u", [P, NT, TOPK], U32)
        ident = sb("ident", [P, P])
        ones_bf = sb("ones_bf", [P, P], BF16)
        tri = sb("tri", [P, P], BF16)
        mask_sum = sb("mask_sum", [P, E], BF16)
        blk_e = sb("blk_e", [P, BC])
        wgs_sb = sb("wgs_sb", [D, INTER])
        wds_sb = sb("wds_sb", [INTER, D])
        tok_idx = sb("tok_idx", [P, 2, TOPK], U32)
        wg_all = sb("wg_all", [D, E, INTER])

        actx = ExitStack()
        with actx:
            def sa(name, shape, dt=F32):
                return sb(name, shape, dt, actx)

            w_raw = sa("w_raw", [D, 3, H * DH])
            w_hi = sa("w_hi", [D, 3, H * DH], F32R)
            w_lo = sa("w_lo", [D, 3, H * DH], F32R)
            wo_sb = sa("wo_sb", [P, G, D])
            bo_sb = sa("bo_sb", [P, TB, D])
            rw_sb = sa("rw_sb", [D, E])
            eb_sb = sa("eb_sb", [P, TB, E])
            zero = sa("zero", [P, 1024])
            ones_row = sa("ones_row", [P, E])
            nb_old = sa("nb_old", [P, E])
            top_old = sa("top_old", [P, E])
            off_old = sa("off_old", [P, E])
            n_taken = sa("n_taken", [P, 1])
            cnt_i = sa("cnt_i", [P, E], I32)
            nb_i = sa("nb_i", [P, E], I32)
            nb_new = sa("nb_new", [P, E])
            taken = sa("taken", [P, E])
            first_new = sa("first_new", [P, E])
            off_new = sa("off_new", [P, E])
            shift = sa("shift", [P, E])
            moved = sa("moved", [P, E])
            beyond = sa("beyond", [P, TB, E])
            shifted = sa("shifted", [P, TB, E])
            offset = sa("offset", [P, TB, E])
            slot1 = sa("slot1", [P, TB, E])
            blk_num = sa("blk_num", [P, BC])
            blk_num_i = sa("blk_num_i", [P, BC], I32)
            le = sa("le", [P, BC, E])
            found = sa("found", [P, BC])
            free = sa("free", [P, BC])
            fix = sa("fix", [P, BC])
            xn1 = sa("xn1", [P, TB, D])
            xnT_hi = sa("xnT_hi", [D, SEQ], F32R)
            xnT_lo = sa("xnT_lo", [D, SEQ], F32R)
            qk_sb = sa("qk_sb", [P, 2, 2, SEQ])
            v_sb = sa("v_sb", [P, 4, TB, P])
            p_sb = sa("p_sb", [P, 2, 2, TB, SEQ])
            pT_sb = sa("pT_sb", [P, 2, 2, TB, SEQ])
            oT_sb = sa("oT_sb", [P, 2, SEQ])
            negmax = sa("negmax", [P, 2, 4])
            rowsum = sa("rowsum", [P, 2, 4])
            rinv = sa("rinv", [P, 2, 4])
            st1 = sa("st1", [P, TB, 6])
            mv1 = sa("mv1", [P, TB, 2])
            ve1 = sa("ve1", [P, TB])
            rs1 = sa("rs1", [P, TB])
            st2 = sa("st2", [P, TB, 6])
            mv2 = sa("mv2", [P, TB, 2])
            ve2 = sa("ve2", [P, TB])
            rs2 = sa("rs2", [P, TB])
            half = sa("half", [P, TB])
            xn2 = sa("xn2", [P, TB, D])
            xn2_src = sa("xn2_src", [P, TB, D])
            xn2T = sa("xn2T", [D, SEQ])
            z_sb = sa("z_sb", [P, TB, E])
            ez_sb = sa("ez_sb", [P, TB, E])
            den = sa("den", [P, TB, E])
            probs = sa("probs", [P, TB, E])
            repl = sa("repl", [P, TB, E])
            mask = sa("mask", [P, TB, E], BF16)
            part_sum = sa("part_sum", [P, E], BF16)
            top_w = sa("top_w", [P, TB, TOPK])
            top_i = sa("top_i", [P, TB, TOPK], U32)
            slot_m = sa("slot_m", [P, TB, E])
            slot8 = sa("slot8", [P, TB, TOPK])
            slot_u = sa("slot_u", [P, TB, TOPK], U32)
            e_of = sa("e_of", [P, TB, TOPK], U32)
            eq = sa("eq", [P, TB, TOPK, TOPK])
            eqw = sa("eqw", [P, TB, TOPK, TOPK])
            w_e = sa("w_e", [P, TB, TOPK])
            wsum = sa("wsum", [P, TB])
            wsc = sa("wsc", [P, TB])
            winv = sa("winv", [P, TB])

        wd_all = sb("wd_all", [P, E // 2, D])
        blk_i = sb("blk_i", [P, NBLK], I32)
        blk_par = sb("blk_par", [P, NBLK], I32)
        blk_pair = sb("blk_pair", [P, NBLK], I32)
        half_i = sb("half_i", [P, 1], I32)
        half_n = sb("half_n", [P, 1], I32)
        half_f = sb("half_f", [P, 1])
        side = sb("side", [P, NBLK])
        side_b = sb("side_b", [P, 2, GB])
        xb = sb("xb", [P, RING, GB, D])
        xbT = sb("xbT", [D, 2, GB, P])
        wg_b = sb("wg_b", [D, 2, GB, P])
        h_b = sb("h_b", [P, 2, GB, P])
        y_b = sb("y_b", [P, 2, GB, D])
        yg = sb("yg", [P, 2, TOPK, D])
        hs = sb("hs", [INTER, 2, P])
        acc = sb("acc", [P, 2, TOPK + 1, D])
        w_t = sb("w_t", [P, 2, TOPK])

        def bank(name, n=1, c=ctx):
            return c.enter_context(nc.psum_tensor(name, [P, n, 512], F32))

        psS = bank("psS", 2)
        psT = bank("psT", 2)
        psQK = bank("psQK")
        psVM = bank("psVM")
        psO = bank("psO")
        psA = bank("psA")

        consts = sem("consts")
        s = {}
        for name in """x0_in x_in w0_in w1_in w2_in c_in wg_in wd_in zfill wqs w_hi_ok w_lo_ok
                ln1_st ln1_ag ln1_ve ln1_rs ln1_xn xt_ps xt_hi xt_lo
                qk_ps qk_ok v_ps v_ok s_ps nm_ok p_ok ri_ok pn_ok t_ps pt_ok o_ps ot_ok ao_ps
                xb_ok x1_ok ln2_st ln2_ag ln2_ve ln2_rs ln2_xn x2t_ps x2t_ok x2r_ok lg_ps z_ok ez_ok den_ok
                pr_ok top_ok rep_ok mask_ok rk_ps sum_ok sm_ok s8_ok su_ok xs_ok eo_ok ti_ok eq_ok eqw_ok
                ws_ok wc_ok wi_ok wn_ok we_ok wr_ok scat
                b_ps b_dve b_pool tab_ok nbi_ok nbs_ok new_ok scan_ok fn_ok of_ok sh_ok by_ok bs_ok sf_ok off_ok s1_ok mv_ok st_ok le_ok fr_ok fx_ok
                be_ok pu_ok
                wg_cp side_cp xt2_ps xt2_ok g_ps h_ok y_ps y_ok
                idx_cp sh_ps hs_ok sho_ps acc_ok wt_ok done""".split():
            s[name] = sem(name)
        ld = [sem(f"load{i}") for i in range(RING)]
        sty = [sem(f"store_y{i}") for i in range(2)]
        gat = [sem(f"gather{i}") for i in range(2)]
        sto = [sem(f"store_out{i}") for i in range(2)]

        def live(b, g, lag, last=NSTEP):
            return not isinstance(b, int) or 0 <= G * b + g - lag < last

        def seq(b, lag):
            return not isinstance(b, int) or 0 <= b - lag < B

        def sequences(eng, body):
            body(0)
            body(1)
            body(2)
            with eng.Fori(3, B) as b:
                body(b)
            body(B)
            body(B + 1)

        block = ctx.enter_context(nc.Block())

        @block.sync
        def _(sp):
            xv = x.rearrange("b s d -> (b s) d").rearrange("(n p) d -> p n d", p=P)
            sp.dma_start(x_res[:, 0:TB, :], xv[:, 0:TB, :]).then_inc(s["x0_in"], 16)
            for i, w in enumerate((wq, wk, wv)):
                sp.dma_start(w_raw[:, i, :], w).then_inc(s[f"w{i}_in"], 16)
            sp.dma_start(x_res[:, TB:NT, :], xv[:, TB:NT, :]).then_inc(s["x_in"], 16)
            sp.dma_start(wo_sb[:], wo.rearrange("(g p) n -> p g n", p=P)).then_inc(s["c_in"], 16)
            sp.dma_start(rw_sb[:], rwT).then_inc(s["c_in"], 16)
            for i in range(TB):
                sp.dma_start(bo_sb[:, i, :], bo.partition_broadcast(P)).then_inc(s["c_in"], 16)
                sp.dma_start(eb_sb[:, i, :], ebias.partition_broadcast(P)).then_inc(s["c_in"], 16)
            sp.dma_start(wgs_sb[:], wgsT).then_inc(s["c_in"], 16)
            sp.dma_start(wds_sb[:], wdsT).then_inc(s["c_in"], 16)
            sp.wait_ge(consts, 5)
            zv = slot_x.rearrange("(p k) d -> p (k d)", p=P).rearrange("p (c n) -> p c n", n=1024)
            nz = zv.shape[1]
            for i in range(4):
                sp.dma_start(zv[:, i * (nz // 4):(i + 1) * (nz // 4), :],
                             zero[:, :].unsqueeze(1).broadcast_to([P, nz // 4, 1024])).then_inc(s["zfill"], 16)
            sp.dma_start(wg_all[:], wgT).then_inc(s["wg_in"], 16)

            sp.wait_ge(s["ao_ps"], NSTEP)
            sp.wait_ge(s["we_ok"], B)
            sp.wait_ge(s["wr_ok"], B)
            sp.wait_ge(s["be_ok"], B)
            sp.wait_ge(s["x2r_ok"], B)
            sp.wait_ge(s["scat"], 16 * NT * TOPK)
            sp.dma_start(wd_all[:], wdT).then_inc(s["wd_in"], 16)

            xv = slot_x.rearrange("(n b p) d -> n p b d", b=GB, p=P)

            def load_group(it, r, first):
                n = RING * it + r
                if not first:
                    sp.wait_ge(s["xt2_ps"], n - RING + 1)
                sp.dma_start(xb[:, r], xv[bass.ds(n, 1)].rearrange("o p b d -> (o p) b d")).then_inc(ld[r], 16)

            for r in range(RING):
                load_group(0, r, True)
            with sp.Fori(1, NGRP // RING) as it:
                for r in range(RING):
                    load_group(it, r, False)

            ov = out.rearrange("b s d -> (b s) d").rearrange("(n p) d -> n p d", p=P)

            def store_out(it, r):
                sp.wait_ge(s["acc_ok"], (2 * it + r + 1) * (TOPK + 1))
                sp.dma_start(ov[bass.ds(2 * it + r, 1)].rearrange("o p d -> (o p) d"), acc[:, r, TOPK, :]).then_inc(sto[r], 16)

            with sp.Fori(0, NT // 2) as it:
                for r in range(2):
                    store_out(it, r)
            for r in range(2):
                sp.wait_ge(sto[r], 16 * (NT // 2))

        @block.tensor
        def _(pe):
            def split_product(dst, wsl, xsl, last):
                for n, (a, c) in enumerate(((0, 0), (0, 1), (1, 0))):
                    m = pe.matmul(dst, wsl[a], xsl[c], start=(n == 0), stop=(n == 2))
                if last is not None:
                    m.then_inc(last, 1)

            def body(b):
                for g in range(G):
                    step = G * b + g
                    if live(b, g, 0):
                        if g == 0:
                            wait(pe, s["xt_hi"], b + 1)
                            wait(pe, s["xt_lo"], b + 1)
                        wait(pe, s["qk_ok"], step)
                        c = slice(g * P, (g + 1) * P)
                        for i in range(2):
                            split_product(psQK[:, 0, i * SEQ:(i + 1) * SEQ], (w_hi[:, i, c], w_lo[:, i, c]),
                                          (xnT_hi[:], xnT_lo[:]), s["qk_ps"] if i == 1 else None)
                    if live(b, g, 1):
                        u = step - 1
                        wait(pe, s["qk_ok"], u + 1)
                        wait(pe, s["p_ok"], 4 * u)
                        for qt in range(TB):
                            for h in range(2):
                                r = slice(h * DH, (h + 1) * DH)
                                m = pe.matmul(psS[:, h, qt * SEQ:(qt + 1) * SEQ],
                                              qk_sb[r, (g - 1) % 2, 0, qt * P:(qt + 1) * P],
                                              qk_sb[r, (g - 1) % 2, 1, :], start=True, stop=True)
                        m.then_inc(s["s_ps"], 1)
                    if live(b, g, 0):
                        wait(pe, s["v_ok"], step)
                        if g == 1 and seq(b, 2):
                            wait(pe, s["sm_ok"], b - 1)
                        if g == 6 and seq(b, 1):
                            wait(pe, s["x2t_ok"], b)
                        if g == 7 and seq(b, 1):
                            wait(pe, s["z_ok"], b)
                        for i in range(TB):
                            r = slice(i * P, (i + 1) * P)
                            c = slice(g * P, (g + 1) * P)
                            split_product(psVM[:, 0, i * P:(i + 1) * P], (xnT_hi[:, r], xnT_lo[:, r]),
                                          (w_hi[:, 2, c], w_lo[:, 2, c]), s["v_ps"] if i == TB - 1 else None)
                    if live(b, g, 3):
                        u = step - 3
                        wait(pe, s["pt_ok"], 2 * u + 2)
                        wait(pe, s["ot_ok"], u)
                        for kt in range(TB):
                            for h in range(2):
                                m = pe.matmul(psO[h * DH:(h + 1) * DH, 0, 0:SEQ],
                                              v_sb[:, (g - 3) % 4, kt, h * DH:(h + 1) * DH],
                                              pT_sb[:, (g - 3) % 2, h, kt, :], start=(kt == 0), stop=(kt == TB - 1))
                        m.then_inc(s["o_ps"], 1)
                    if live(b, g, 2):
                        u = step - 2
                        for h in range(2):
                            wait(pe, s["pn_ok"], 4 * u + 2 * h + 2)
                            wait(pe, s["pt_ok"], 2 * u - 1 + h)
                            for qt in range(TB):
                                for kt in range(TB):
                                    m = pe.transpose(psT[:, h, kt * SEQ + qt * P:kt * SEQ + (qt + 1) * P],
                                                     p_sb[:, (g - 2) % 2, h, qt, kt * P:(kt + 1) * P], ident[:])
                            m.then_inc(s["t_ps"], 1)
                    if live(b, g, 4):
                        u = step - 4
                        wait(pe, s["ot_ok"], u + 1)
                        gp = (g - 4) % G
                        if gp == 0:
                            wait(pe, s["x1_ok"], b)
                        for i in range(TB):
                            m = pe.matmul(psA[:, 0, i * P:(i + 1) * P], oT_sb[:, (g - 4) % 2, i * P:(i + 1) * P],
                                          wo_sb[:, gp, :], start=(gp == 0 and i == 0), stop=(gp == G - 1),
                                          skip_group_check=True)
                        m.then_inc(s["ao_ps"], 1)
                    if g == 0 and seq(b, 2):
                        values_read(b, step)
                        wait(pe, s["mask_ok"], b - 1)
                        wait(pe, s["sum_ok"], b - 1)
                        ranks(b)
                    if g == 5 and seq(b, 1):
                        values_read(b, step)
                        if seq(b, 2):
                            wait(pe, s["sm_ok"], b - 1)
                        wait(pe, s["ln2_xn"], TB * b)
                        for i in range(TB):
                            m = pe.transpose(psVM[:, 0, i * P:(i + 1) * P], xn2[:, i, :], ident[:])
                        m.then_inc(s["x2t_ps"], 1)
                    if g == 6 and seq(b, 1):
                        values_read(b, step)
                        wait(pe, s["x2t_ok"], b)
                        for i in range(TB):
                            m = pe.matmul(psVM[:, 0, i * E:(i + 1) * E], xn2T[:, i * P:(i + 1) * P], rw_sb[:],
                                          start=True, stop=True)
                        m.then_inc(s["lg_ps"], 1)
                    if g == 7 and live(b, g, 0):
                        values_read(b, step)
                        input_transpose(b + 1)

            def values_read(b, step):
                if live(b, 0, 0):
                    wait(pe, s["v_ok"], step + 1)

            def ranks(b):
                for i in range(TB):
                    o = psVM[:, 0, i * E:(i + 1) * E]
                    pe.matmul(o, tri[:], mask[:, i, :], start=True, stop=False)
                    for j in range(i):
                        pe.matmul(o, ones_bf[:], mask[:, j, :], start=False, stop=False)
                    pe.matmul(o, ones_bf[:], mask_sum[:], start=False, stop=True)
                o = psVM[:, 0, TB * E:(TB + 1) * E]
                pe.matmul(o, ones_bf[:], mask_sum[:], start=True, stop=False)
                for j in range(TB):
                    m = pe.matmul(o, ones_bf[:], mask[:, j, :], start=False, stop=(j == TB - 1))
                m.then_inc(s["rk_ps"], 1)

            def input_transpose(b):
                wait(pe, s["ln1_xn"], TB * (b + 1))
                for i in range(TB):
                    m = pe.transpose(psVM[:, 0, i * P:(i + 1) * P], xn1[:, i, :], ident[:])
                m.then_inc(s["xt_ps"], 1)

            pe.wait_ge(consts, 5)
            input_transpose(0)
            pe.wait_ge(s["w_hi_ok"], 3)
            pe.wait_ge(s["w_lo_ok"], 3)
            pe.wait_ge(s["c_in"], 16 * (4 + 2 * TB))
            sequences(pe, body)

            pe.wait_ge(s["be_ok"], B)
            pe.wait_ge(s["z_ok"], B)
            for c in range(BC):
                n = min(P, NBLK - c * P)
                m = pe.matmul(psQK[:, 0, c * P:c * P + n], blk_e[:, c:c + 1].broadcast_to([P, P]), ident[:, 0:n],
                              start=True, stop=True)
            m.then_inc(s["b_ps"], 1)
            pe.wait_ge(s["tab_ok"], 2)
            pe.wait_ge(s["wd_in"], 16)

            def transposes(it, r, n):
                par = r % 2
                pe.wait_ge(ld[r], 16 * (it + 1))
                wait(pe, s["xt2_ok"], n - 1)
                for i in range(GB):
                    m = pe.transpose(psT[:, par, i * P:(i + 1) * P], xb[:, r, i, :], ident[:])
                m.then_inc(s["xt2_ps"], 1)

            def gates(r, n):
                par = r % 2
                pe.wait_ge(s["xt2_ok"], n + 1)
                pe.wait_ge(s["wg_cp"], n + 1)
                wait(pe, s["h_ok"], GB * (n - 1))
                for i in range(GB):
                    m = pe.matmul(psS[:, par, i * P:(i + 1) * P], wg_b[:, par, i, :], xbT[:, par, i, :], start=True, stop=True)
                m.then_inc(s["g_ps"], 1)

            def downs(r, n):
                par = r % 2
                ps = (psQK, psVM)[par]
                pe.wait_ge(s["h_ok"], GB * (n + 1))
                wait(pe, s["y_ok"], n - 1)
                for i in range(GB):
                    pair = pe.value_load(blk_pair[0:1, bass.ds(n * GB + i, 1)], min_val=0, max_val=E // 2 - 1)
                    m = pe.matmul(ps[:, 0, i * P:(i + 1) * P], h_b[:, par, i, :],
                                  wd_all[:, bass.ds(pair, 1), :].rearrange("p o d -> p (o d)"), start=True, stop=True)
                m.then_inc(s["y_ps"], 1)

            def experts(it, first):
                for r in range(RING):
                    n = RING * it + r
                    transposes(it, r, n)
                    if not (first and r < 1):
                        gates((r - 1) % RING, n - 1)
                    if not (first and r < 2):
                        downs((r - 2) % RING, n - 2)

            experts(0, True)
            with pe.Fori(1, NGRP // RING) as it:
                experts(it, False)
            gates(RING - 1, NGRP - 1)
            downs(RING - 2, NGRP - 2)
            downs(RING - 1, NGRP - 1)

            def shared(it, r, first):
                n = 2 * it + r
                if not first:
                    pe.wait_ge(s["hs_ok"], n - 1)
                    pe.wait_ge(s["acc_ok"], (TOPK + 1) * (n - 2) + 1)
                pe.matmul((psO, psA)[r][0:INTER, 0, 0:P], wgs_sb[:], xn2T_res[:, bass.ds(n * P, P)],
                          start=True, stop=True).then_inc(s["sh_ps"], 1)
                pe.wait_ge(s["hs_ok"], n + 1)
                pe.matmul(psT[:, r, 0:P], hs[:, r, :], wds_sb[:], start=True, stop=True).then_inc(s["sho_ps"], 1)

            shared(0, 0, True)
            shared(0, 1, True)
            with pe.Fori(1, NT // 2) as it:
                shared(it, 0, False)
                shared(it, 1, False)

        @block.scalar
        def _(act):
            for i in range(3):
                act.wait_ge(s[f"w{i}_in"], 16)
                act.activation(w_hi[:, i, :], w_raw[:, i, :], ACT.Copy, scale=DH ** -0.5 if i == 0 else 1.0).then_inc(s["w_hi_ok"], 1)

            def body(b):
                for g in range(G):
                    step = G * b + g
                    if live(b, g, 0):
                        wait(act, s["qk_ps"], step + 1)
                        wait(act, s["s_ps"], step - 1)
                        act.copy(qk_sb[:, g % 2].rearrange("p a t -> p (a t)"), psQK[:, 0, :]).then_inc(s["qk_ok"], 1)
                        wait(act, s["v_ps"], step + 1)
                        wait(act, s["o_ps"], step - 3)
                        act.copy(v_sb[:, g % 4].rearrange("p t d -> p (t d)"), psVM[:, 0, 0:TB * P]).then_inc(s["v_ok"], 1)
                    if live(b, g, 1):
                        u = step - 1
                        wait(act, s["nm_ok"], u + 1)
                        wait(act, s["t_ps"], 2 * u - 2)
                        wait(act, s["ri_ok"], u - 1)
                        for h in range(2):
                            for qt in range(TB):
                                k = 2 * h + qt
                                act.activation(p_sb[:, (g - 1) % 2, h, qt, :], psS[:, h, qt * SEQ:(qt + 1) * SEQ], ACT.Exp,
                                               bias=negmax[:, (g - 1) % 2, k:k + 1], scale=1.0,
                                               accum_out=rowsum[:, (g - 1) % 2, k:k + 1]).then_inc(s["p_ok"], 1)
                    if g == 7 and seq(b, 1):
                        wait(act, s["z_ok"], b)
                        wait(act, s["den_ok"], b - 1)
                        act.activation(ez_sb[:], z_sb[:], ACT.Exp, scale=-1.0).then_inc(s["ez_ok"], 1)
                    if g == 7 and seq(b, 1):
                        wait(act, s["x2t_ok"], b)
                        act.copy(xn2T_res[:, bass.ds((b - 1) * SEQ, SEQ)], xn2T[:]).then_inc(s["x2r_ok"], 1)

            sequences(act, body)

            def evac(r, n):
                par = r % 2
                act.wait_ge(s["xt2_ps"], n + 1)
                wait(act, s["g_ps"], n - 1)
                act.copy(xbT[:, par].rearrange("p a t -> p (a t)"), psT[:, par, :]).then_inc(s["xt2_ok"], 1)

            def silu(r, n):
                par = r % 2
                act.wait_ge(s["g_ps"], n + 1)
                wait(act, s["y_ps"], n - 1)
                act.wait_ge(s["side_cp"], n + 1)
                for i in range(GB):
                    act.activation(h_b[:, par, i, :], psS[:, par, i * P:(i + 1) * P], ACT.Silu,
                                   scale=side_b[:, par, i:i + 1]).then_inc(s["h_ok"], 1)

            def store_y(r, n, it):
                par = r % 2
                act.wait_ge(s["y_ok"], n + 1)
                act.dma_start(block_y.rearrange("(n b p) d -> n p b d", b=GB, p=P)[bass.ds(n, 1)].rearrange("o p b d -> (o p) b d"),
                              y_b[:, par]).then_inc(sty[par], 16)

            def experts(it, first):
                for r in range(RING):
                    n = RING * it + r
                    evac(r, n)
                    if not (first and r < 1):
                        silu((r - 1) % RING, n - 1)
                    if not (first and r < 3):
                        store_y((r - 3) % RING, n - 3, it)

            experts(0, True)
            with act.Fori(1, NGRP // RING) as it:
                experts(it, False)
            silu(RING - 1, NGRP - 1)
            for k in (3, 2, 1):
                store_y(RING - k, NGRP - k, None)

            def shared(it, r, first):
                n = 2 * it + r
                act.wait_ge(s["sh_ps"], n + 1)
                if not first:
                    act.wait_ge(s["sho_ps"], n - 1)
                act.activation(hs[:, r, :], (psO, psA)[r][0:INTER, 0, 0:P], ACT.Silu).then_inc(s["hs_ok"], 1)

            shared(0, 0, True)
            shared(0, 1, True)
            with act.Fori(1, NT // 2) as it:
                shared(it, 0, False)
                shared(it, 1, False)

        @block.gpsimd
        def _(pool):
            held[pool] = pool.alloc_register("pool_wait")
            pool.memset(ident[:], 0.0).then_inc(s["b_pool"], 1)
            pool.wait_ge(s["b_pool"], 1)
            pool.affine_select(out=ident[:], in_=ident[:], compare_op=ALU.not_equal, fill=1.0, base=0,
                               pattern=[[-1, P]], channel_multiplier=1).then_inc(consts, 1)
            pool.memset(half[:], -0.5).then_inc(consts, 1)
            pool.memset(zero[:], 0.0).then_inc(consts, 1)
            pool.memset(ones_bf[:], 1.0).then_inc(consts, 1)
            pool.memset(x_res[:, NT:NT + TB, :], 0.0).then_inc(consts, 1)
            pool.wait_ge(consts, 5)
            pool.wait_ge(s["ln1_ve"], 1)
            pool.tensor_tensor(rs1[:], ve1[:], half[:], ALU.pow).then_inc(s["ln1_rs"], 1)
            pool.memset(tri[:], 0.0).then_inc(s["b_pool"], 1)
            for t in (nb_old, top_old, off_old, n_taken):
                pool.memset(t[:], 0.0).then_inc(s["b_pool"], 1)
            pool.memset(blk_e[:], float(E)).then_inc(s["b_pool"], 1)
            pool.memset(ones_row[:], 1.0).then_inc(s["b_pool"], 1)
            pool.memset(mask_sum[:], 0.0).then_inc(s["sum_ok"], 1)
            pool.wait_ge(s["b_pool"], 8)
            pool.affine_select(out=tri[:], in_=tri[:], compare_op=ALU.is_ge, fill=1.0, base=0,
                               pattern=[[-1, P]], channel_multiplier=1).then_inc(s["b_pool"], 1)
            pool.iota(blk_num_i[:], pattern=[[P, BC]], base=0, channel_multiplier=1).then_inc(s["b_pool"], 1)

            def body(b):
                for g in range(G):
                    step = G * b + g
                    if g == 1 and seq(b, 2):
                        wait_apart(pool, s["mask_ok"], b - 1)
                        wait_apart(pool, s["scat"], 16 * TB * TOPK * (b - 2))
                        pool.tensor_scalar(xn2_src[:], xn2[:], 1.0, 1.0, ALU.mult, ALU.mult).then_inc(s["xs_ok"], 1)
                    if live(b, g, 2):
                        u = step - 2
                        wait_apart(pool, s["ri_ok"], u + 1)
                        for h in range(2):
                            for qt in range(TB):
                                k = 2 * h + qt
                                pq = p_sb[:, (g - 2) % 2, h, qt, :]
                                pool.tensor_scalar(pq, pq, rinv[:, (g - 2) % 2, k:k + 1], 1.0, ALU.mult, ALU.mult).then_inc(s["pn_ok"], 1)
                    if g == 3 and (isinstance(b, int) and b < B or not isinstance(b, int)):
                        wait(pool, s["ln1_ve"], b + 2)
                        pool.tensor_tensor(rs1[:], ve1[:], half[:], ALU.pow).then_inc(s["ln1_rs"], 1)
                    if g == 2 and live(b, g, 0):
                        if isinstance(b, int) and b == 0:
                            pool.wait_ge(s["c_in"], 16 * (4 + 2 * TB))
                        wait(pool, s["ln1_xn"], TB * (b + 1))
                        xr = x_res[:, bass.ds(b * TB, TB), :]
                        pool.tensor_tensor(xr, xr, bo_sb[:], ALU.add).then_inc(s["xb_ok"], 1)
                    if g == 4 and seq(b, 1):
                        wait(pool, s["ln2_ve"], b)
                        pool.tensor_tensor(rs2[:], ve2[:], half[:], ALU.pow).then_inc(s["ln2_rs"], 1)
                    if SCAT[g] and seq(b, 2):
                        if g == 2:
                            wait_apart(pool, s["su_ok"], b - 1)
                            wait_apart(pool, s["xs_ok"], b - 1)
                            if isinstance(b, int) and b == 2 or not isinstance(b, int):
                                pool.wait_ge(s["zfill"], 16 * 4)
                        k0 = sum(SCAT[:g])
                        for k in range(k0, k0 + SCAT[g]):
                            i, j = k // TOPK, k % TOPK
                            pool.indirect_dma_start(slot_x, bass.IndirectOffsetOnAxis(ap=slot_u[:, i, j:j + 1], axis=0),
                                                    xn2_src[:, i, :], None).then_inc(s["scat"], 16)

            sequences(pool, body)

            pool.wait_ge(s["be_ok"], B)
            pool.wait_ge(s["wr_ok"], B)
            pool.wait_ge(s["x2r_ok"], B)
            pool.wait_ge(s["ao_ps"], NSTEP)
            pool.wait_ge(s["scat"], 16 * NT * TOPK)
            pool.iota(half_i[:], pattern=[[0, 1]], base=0, channel_multiplier=1).then_inc(s["b_pool"], 1)

            pool.wait_ge(sty[0], 16 * NGRP // 2)
            pool.wait_ge(sty[1], 16 * NGRP // 2)

            def gather(it, r, first):
                n = 2 * it + r
                if not first:
                    pool.wait_ge(s["acc_ok"], (n - 1) * (TOPK + 1))
                    pool.wait_ge(gat[r], 16 * TOPK * it)
                pool.tensor_copy(tok_idx[:, r, :], pos_u[:, bass.ds(n, 1), :].rearrange("p o k -> p (o k)")).then_inc(s["idx_cp"], 1)
                wait_apart(pool, s["idx_cp"], n + 1)
                for k in range(TOPK):
                    pool.indirect_dma_start(yg[:, r, k, :], None, block_y,
                                            bass.IndirectOffsetOnAxis(ap=tok_idx[:, r, k:k + 1], axis=0)).then_inc(gat[r], 16)

            gather(0, 0, True)
            gather(0, 1, True)
            with pool.Fori(1, NT // 2) as it:
                gather(it, 0, False)
                gather(it, 1, False)

        @block.vector
        def _(dve):
            def ln_stats(b, which, st, mv, ve):
                if which == "ln2":
                    wait_apart(dve, s["x1_ok"], b + 1)
                for i in range(TB):
                    src = x_res[:, bass.ds(b * TB + i, 1), :].rearrange("p o d -> p (o d)")
                    m = dve.bn_stats(st[:, i, :], src)
                m.then_inc(s[which + "_st"], 1)
                wait_apart(dve, s[which + "_st"], b + 1)
                for i in range(TB):
                    m = dve.bn_aggr(mv[:, i, :], st[:, i, :])
                m.then_inc(s[which + "_ag"], 1)
                wait(dve, s[which + "_ag"], b + 1)
                dve.tensor_scalar(ve[:], mv[:, :, 1], EPS, None, ALU.add).then_inc(s[which + "_ve"], 1)

            def ln_apply(b, which, dst, mv, rs):
                wait(dve, s[which + "_rs"], b + 1)
                for i in range(TB):
                    src = x_res[:, bass.ds(b * TB + i, 1), :].rearrange("p o d -> p (o d)")
                    dve.tensor_scalar(dst[:, i, :], src, mv[:, i, 0:1], rs[:, i:i + 1], ALU.subtract,
                                      ALU.mult).then_inc(s[which + "_xn"], 1)

            def input_split(b):
                wait(dve, s["xt_ps"], b + 1)
                wait(dve, s["v_ps"], G * b)
                dve.tensor_copy(xnT_hi[:], psVM[:, 0, 0:SEQ]).then_inc(s["xt_hi"], 1)
                wait(dve, s["xt_hi"], b + 1)
                dve.tensor_tensor(xnT_lo[:], psVM[:, 0, 0:SEQ], xnT_hi[:].bitcast(F32), ALU.subtract).then_inc(s["xt_lo"], 1)

            held[dve] = dve.alloc_register("dve_wait")
            dve.wait_ge(s["x0_in"], 16)
            ln_stats(0, "ln1", st1, mv1, ve1)
            ln_apply(0, "ln1", xn1, mv1, rs1)
            input_split(0)
            for i in range(3):
                dve.wait_ge(s["w_hi_ok"], i + 1)
                dve.scalar_tensor_tensor(out=w_lo[:, i, :], in0=w_raw[:, i, :], scalar=DH ** -0.5 if i == 0 else 1.0,
                                         in1=w_hi[:, i, :].bitcast(F32), op0=ALU.mult, op1=ALU.subtract).then_inc(s["w_lo_ok"], 1)
            dve.wait_ge(s["x_in"], 16)
            dve.wait_ge(consts, 5)
            dve.wait_ge(s["b_pool"], 10)
            dve.tensor_copy(blk_num[:], blk_num_i[:]).then_inc(s["b_dve"], 1)
            dve.wait_ge(s["b_dve"], 1)
            dve.wait_ge(s["c_in"], 16 * (4 + 2 * TB))

            def choose(b):
                n = b - 1
                wait(dve, s["ez_ok"], n)
                dve.tensor_scalar(den[:], ez_sb[:], 1.0, None, ALU.add).then_inc(s["den_ok"], 1)
                wait(dve, s["den_ok"], n)
                dve.reciprocal(probs[:], den[:]).then_inc(s["pr_ok"], 1)
                wait_apart(dve, s["pr_ok"], n)
                for i in range(TB):
                    m = dve.max(top_w[:, i, :], probs[:, i, :])
                m.then_inc(s["top_ok"], 1)
                wait_apart(dve, s["top_ok"], n)
                for i in range(TB):
                    m = dve.match_replace(repl[:, i, :], top_w[:, i, :], probs[:, i, :], -1.0)
                m.then_inc(s["rep_ok"], 1)
                wait(dve, s["rep_ok"], n)
                dve.tensor_tensor(mask[:], probs[:], repl[:], ALU.not_equal).then_inc(s["mask_ok"], 1)

            def slots(b):
                n = b - 1
                last = TB * E
                rank = psVM[:, 0, 0:last].rearrange("p (i e) -> p i e", i=TB)
                row = lambda t: t[:].unsqueeze(1).broadcast_to([P, TB, E])
                wait(dve, s["rk_ps"], n)
                dve.tensor_scalar(cnt_i[:], psVM[:, 0, last:last + E], float(P - 1), None, ALU.add).then_inc(s["nbi_ok"], 1)
                wait(dve, s["st_ok"], 4 * (n - 1))
                dve.tensor_tensor(beyond[:], rank, row(top_old), ALU.is_ge).then_inc(s["by_ok"], 1)
                wait(dve, s["nbi_ok"], n)
                dve.tensor_scalar(nb_i[:], cnt_i[:], P.bit_length() - 1, None, ALU.logical_shift_right).then_inc(s["nbs_ok"], 1)
                part_counts(n)
                wait(dve, s["nbs_ok"], n)
                dve.tensor_tensor(nb_new[:], nb_i[:], nb_old[:], ALU.subtract).then_inc(s["new_ok"], 1)
                wait(dve, s["new_ok"], n)
                dve.tensor_tensor_scan(taken[:], ones_row[:], nb_new[:], n_taken[:, 0:1], ALU.mult, ALU.add).then_inc(s["scan_ok"], 1)
                wait(dve, s["scan_ok"], n)
                dve.tensor_tensor(first_new[:], taken[:], nb_new[:], ALU.subtract).then_inc(s["fn_ok"], 1)
                wait(dve, s["fn_ok"], n)
                dve.tensor_tensor(off_new[:], first_new[:], nb_old[:], ALU.subtract).then_inc(s["of_ok"], 1)
                wait(dve, s["of_ok"], n)
                dve.scalar_tensor_tensor(out=shift[:], in0=off_new[:], scalar=float(P), in1=off_old[:], op0=ALU.mult,
                                         op1=ALU.subtract).then_inc(s["sh_ok"], 1)
                wait(dve, s["sh_ok"], n)
                wait(dve, s["by_ok"], n)
                dve.tensor_tensor(shifted[:], beyond[:], row(shift), ALU.mult).then_inc(s["bs_ok"], 1)
                dve.scalar_tensor_tensor(out=moved[:], in0=nb_new[:], scalar=0.5, in1=shift[:], op0=ALU.is_gt,
                                         op1=ALU.mult).then_inc(s["mv_ok"], 1)
                wait(dve, s["bs_ok"], n)
                dve.tensor_tensor(offset[:], shifted[:], row(off_old), ALU.add).then_inc(s["off_ok"], 1)
                wait(dve, s["off_ok"], n)
                dve.scalar_tensor_tensor(out=slot1[:], in0=rank, scalar=1.0, in1=offset[:], op0=ALU.add,
                                         op1=ALU.add).then_inc(s["s1_ok"], 1)
                wait(dve, s["s1_ok"], n)
                dve.tensor_tensor(slot_m[:], slot1[:], mask[:], ALU.mult).then_inc(s["sm_ok"], 1)
                wait(dve, s["mv_ok"], n)
                dve.tensor_tensor(off_old[:], off_old[:], moved[:], ALU.add).then_inc(s["st_ok"], 1)
                dve.tensor_copy(nb_old[:], nb_i[:]).then_inc(s["st_ok"], 1)
                dve.tensor_scalar(top_old[:], nb_i[:], float(P), None, ALU.mult).then_inc(s["st_ok"], 1)
                dve.tensor_copy(n_taken[:], taken[:, E - 1:E]).then_inc(s["st_ok"], 1)
                wait_apart(dve, s["sm_ok"], n)
                for i in range(TB):
                    m = dve.max(slot8[:, i, :], slot_m[:, i, :])
                m.then_inc(s["s8_ok"], 1)
                wait(dve, s["s8_ok"], n)
                wait(dve, s["scat"], 16 * TB * TOPK * (b - 2))
                dve.tensor_scalar(slot_u[:], slot8[:], -1.0, None, ALU.add).then_inc(s["su_ok"], 1)
                for i in range(TB):
                    m = dve.max_index(e_of[:, i, :], slot8[:, i, :], slot_m[:, i, :])
                m.then_inc(s["eo_ok"], 1)
                wait(dve, s["su_ok"], n)
                dve.tensor_copy(pos_u[:, bass.ds((b - 2) * TB, TB), :], slot_u[:]).then_inc(s["pu_ok"], 1)

            def part_counts(n):
                wait(dve, s["sum_ok"], n)
                dve.tensor_tensor(part_sum[:], mask_sum[:], mask[:, 0, :], ALU.add).then_inc(s["ws_ok"], 1)
                wait(dve, s["ws_ok"], n)
                dve.tensor_tensor(mask_sum[:], part_sum[:], mask[:, 1, :], ALU.add).then_inc(s["sum_ok"], 1)

            def blocks(b):
                n = b - 1
                for c in range(BC):
                    m = dve.tensor_scalar(le[:, c, :], taken[:], blk_num[:, c:c + 1], None, ALU.is_le, ALU.add,
                                          accum_out=found[:, c:c + 1])
                m.then_inc(s["le_ok"], 1)
                wait(dve, s["be_ok"], n - 1)
                dve.tensor_scalar(free[:], blk_e[:], E - 0.5, None, ALU.is_gt).then_inc(s["fr_ok"], 1)
                wait(dve, s["fr_ok"], n)
                wait(dve, s["le_ok"], n)
                dve.scalar_tensor_tensor(out=fix[:], in0=found[:], scalar=-float(E), in1=free[:], op0=ALU.add,
                                         op1=ALU.mult).then_inc(s["fx_ok"], 1)
                wait(dve, s["fx_ok"], n)
                dve.tensor_tensor(blk_e[:], blk_e[:], fix[:], ALU.add).then_inc(s["be_ok"], 1)

            def weights(b):
                n = b - 1
                for i in range(TB):
                    m = dve.max_index(top_i[:, i, :], top_w[:, i, :], probs[:, i, :])
                m.then_inc(s["ti_ok"], 1)
                wait(dve, s["ti_ok"], n)
                wait(dve, s["eo_ok"], n)
                shape = [P, TB, TOPK, TOPK]
                dve.tensor_tensor(eq[:], e_of[:].unsqueeze(3).broadcast_to(shape),
                                  top_i[:].unsqueeze(2).broadcast_to(shape), ALU.is_equal).then_inc(s["eq_ok"], 1)
                dve.tensor_reduce(wsum[:], top_w[:], AX.X, ALU.add).then_inc(s["wc_ok"], 1)
                wait(dve, s["eq_ok"], n)
                dve.tensor_tensor(eqw[:], eq[:], top_w[:].unsqueeze(2).broadcast_to(shape), ALU.mult).then_inc(s["eqw_ok"], 1)
                wait(dve, s["wc_ok"], n)
                dve.tensor_scalar(wsc[:], wsum[:], 1e-9, 1.0 / ROUTED_SCALE, ALU.add, ALU.mult).then_inc(s["wi_ok"], 1)
                wait(dve, s["eqw_ok"], n)
                dve.tensor_reduce(w_e[:], eqw[:], AX.X, ALU.add).then_inc(s["we_ok"], 1)
                wait(dve, s["wi_ok"], n)
                dve.reciprocal(winv[:], wsc[:]).then_inc(s["wn_ok"], 1)
                wait(dve, s["wn_ok"], n)
                wait(dve, s["we_ok"], n)
                dve.tensor_tensor(wE_res[:, bass.ds((b - 2) * TB, TB), :], w_e[:],
                                  winv[:].unsqueeze(2).broadcast_to([P, TB, TOPK]), ALU.mult).then_inc(s["wr_ok"], 1)

            def body(b):
                for g in range(G):
                    step = G * b + g
                    if live(b, g, 2):
                        u = step - 2
                        wait(dve, s["p_ok"], 4 * u + 4)
                        wait(dve, s["pn_ok"], 4 * u - 4)
                        dve.reciprocal(rinv[:, (g - 2) % 2, :], rowsum[:, (g - 2) % 2, :]).then_inc(s["ri_ok"], 1)
                    if g == 0 and seq(b, 2):
                        choose(b)
                    if g == 1 and seq(b, 2):
                        slots(b)
                    if g == 2 and seq(b, 2):
                        weights(b)
                    if g == 3 and seq(b, 2):
                        blocks(b)
                    if g == 3 and live(b, g, 0):
                        ln_stats(b + 1, "ln1", st1, mv1, ve1)
                    if g == 4 and seq(b, 1):
                        wait(dve, s["ao_ps"], G * b)
                        wait(dve, s["xb_ok"], b)
                        xr = x_res[:, bass.ds((b - 1) * TB, TB), :]
                        dve.tensor_tensor(xr, psA[:, 0, 0:SEQ].rearrange("p (i d) -> p i d", i=TB), xr, ALU.add).then_inc(s["x1_ok"], 1)
                        ln_stats(b - 1, "ln2", st2, mv2, ve2)
                    if g == 5 and seq(b, 1):
                        wait(dve, s["x2t_ps"], b - 1)
                        wait(dve, s["xs_ok"], b - 1)
                        ln_apply(b - 1, "ln2", xn2, mv2, rs2)
                    if g == 6 and seq(b, 1):
                        wait(dve, s["x2t_ps"], b)
                        wait(dve, s["lg_ps"], b - 1)
                        wait(dve, s["x2r_ok"], b - 1)
                        dve.tensor_copy(xn2T[:], psVM[:, 0, 0:SEQ]).then_inc(s["x2t_ok"], 1)
                    if g == 6 and live(b, g, 0):
                        wait(dve, s["xt_ps"], b + 1)
                        ln_apply(b + 1, "ln1", xn1, mv1, rs1)
                    if g == 7 and seq(b, 1):
                        wait(dve, s["lg_ps"], b)
                        wait(dve, s["ez_ok"], b - 1)
                        dve.tensor_tensor(z_sb[:], psVM[:, 0, 0:TB * E].rearrange("p (i e) -> p i e", i=TB), eb_sb[:], ALU.add).then_inc(s["z_ok"], 1)
                    if live(b, g, 1):
                        u = step - 1
                        wait(dve, s["s_ps"], u + 1)
                        wait(dve, s["p_ok"], 4 * u - 4)
                        dve.tensor_reduce(negmax[:, (g - 1) % 2, :], psS[:, :, :].rearrange("p h (q k) -> p (h q) k", q=TB),
                                          AX.X, ALU.max, negate=True).then_inc(s["nm_ok"], 1)
                    if live(b, g, 3):
                        u = step - 3
                        wait(dve, s["o_ps"], u + 1)
                        wait(dve, s["ao_ps"], u - 1)
                        dve.tensor_copy(oT_sb[:, (g - 3) % 2, :], psO[:, 0, 0:SEQ]).then_inc(s["ot_ok"], 1)
                    if g == 7 and live(b, g, 0):
                        input_split(b + 1)
                    if live(b, g, 2):
                        u = step - 2
                        for h in range(2):
                            wait(dve, s["t_ps"], 2 * u + h + 1)
                            wait(dve, s["o_ps"], u - 1)
                            dve.tensor_copy(pT_sb[:, (g - 2) % 2, h].rearrange("p a t -> p (a t)"), psT[:, h, :]).then_inc(s["pt_ok"], 1)

            sequences(dve, body)

            dve.wait_ge(s["b_pool"], 11)
            k = [1]

            def link(m):
                k[0] += 1
                m.then_inc(s["b_dve"], 1)
                dve.wait_ge(s["b_dve"], k[0])

            link(dve.tensor_scalar(half_n[:], half_i[:], INTER.bit_length() - 1, None, ALU.logical_shift_right))
            link(dve.tensor_copy(half_f[:], half_n[:]))
            dve.wait_ge(s["b_ps"], 1)
            link(dve.tensor_scalar(blk_i[:], psQK[:, 0, 0:NBLK], float(E - 1), None, ALU.min))
            dve.tensor_scalar(blk_pair[:], blk_i[:], 1, None, ALU.logical_shift_right).then_inc(s["tab_ok"], 1)
            link(dve.tensor_scalar(blk_par[:], blk_i[:], 1, None, ALU.bitwise_and))
            dve.tensor_scalar(side[:], blk_par[:], half_f[:, 0:1], None, ALU.is_equal).then_inc(s["tab_ok"], 1)
            dve.wait_ge(s["tab_ok"], 2)

            dve.wait_ge(s["wg_in"], 16)

            def gate_weights(r, n, first):
                par = r % 2
                if not (first and r < 2):
                    dve.wait_ge(s["g_ps"], n - 1)
                    dve.wait_ge(s["h_ok"], GB * (n - 1))
                for i in range(GB):
                    pair = dve.value_load(blk_pair[0:1, bass.ds(n * GB + i, 1)], min_val=0, max_val=E // 2 - 1)
                    m = dve.tensor_copy(wg_b[:, par, i, :].rearrange("p (k i) -> p k i", k=2), wg_all[:, bass.ds(2 * pair, 2), :])
                m.then_inc(s["wg_cp"], 1)
                dve.tensor_copy(side_b[:, par, :], side[:, bass.ds(n * GB, GB)]).then_inc(s["side_cp"], 1)

            def outputs(r, n, first):
                par = r % 2
                dve.wait_ge(s["y_ps"], n + 1)
                if not first:
                    dve.wait_ge(sty[par], 8 * (n - par))
                dve.tensor_copy(y_b[:, par].rearrange("p a d -> p (a d)"), (psQK, psVM)[par][:, 0, :]).then_inc(s["y_ok"], 1)

            def experts(it, first):
                for r in range(RING):
                    n = RING * it + r
                    gate_weights(r, n, first)
                    if not (first and r < 2):
                        outputs((r - 2) % RING, n - 2, first)

            experts(0, True)
            with dve.Fori(1, NGRP // RING) as it:
                experts(it, False)
            outputs(RING - 2, NGRP - 2, False)
            outputs(RING - 1, NGRP - 1, False)

            def combine(it, r, first):
                n = 2 * it + r
                c = (TOPK + 1) * n
                dve.tensor_copy(w_t[:, r, :], wE_res[:, bass.ds(n, 1), :].rearrange("p o k -> p (o k)")).then_inc(s["wt_ok"], 1)
                if not first:
                    dve.wait_ge(sto[r], 16 * it)
                dve.wait_ge(s["sho_ps"], n + 1)
                dve.tensor_tensor(acc[:, r, 0, :], psT[:, r, 0:P], x_res[:, bass.ds(n, 1), :].rearrange("p o d -> p (o d)"),
                                  ALU.add).then_inc(s["acc_ok"], 1)
                dve.wait_ge(s["wt_ok"], n + 1)
                dve.wait_ge(gat[r], 16 * TOPK * (it + 1))
                for k_ in range(TOPK):
                    dve.wait_ge(s["acc_ok"], c + k_ + 1)
                    dve.scalar_tensor_tensor(out=acc[:, r, k_ + 1, :], in0=yg[:, r, k_, :], scalar=w_t[:, r, k_:k_ + 1],
                                             in1=acc[:, r, k_, :], op0=ALU.mult, op1=ALU.add).then_inc(s["acc_ok"], 1)

            combine(0, 0, True)
            combine(0, 1, True)
            with dve.Fori(1, NT // 2) as it:
                combine(it, 0, False)
                combine(it, 1, False)


_OUTS = [((B, SEQ, D), "float32")]


def kernel(**inputs):
    import numpy as _np
    import concourse.bacc as _bacc
    from concourse import mybir as _mybir
    from concourse.bass_utils import run_bass_kernel_spmd as _run

    pre = {k.replace("L0_attn_", "").replace("L0_ffn_", ""): _np.asarray(v) for k, v in inputs.items()}
    given = {
        "x": pre["x"], "Wq": pre["Wq"], "Wk": pre["Wk"], "Wv": pre["Wv"], "Wo": pre["Wo"], "bo": pre["bo"],
        "rwT": pre["router_w"].T, "ebias": pre["expert_bias"],
        "wgT": pre["w_gate"].transpose(2, 0, 1),
        "wdT": pre["w_down"].reshape(E // 2, 2, D, INTER).transpose(1, 3, 0, 2).reshape(P, E // 2, D),
        "wgsT": pre["w_gate_shared"].T, "wdsT": pre["w_down_shared"].T,
    }
    nc = _bacc.Bacc("TRN2", target_bir_lowering=False, num_devices=1)
    arrays, args = {}, []
    for name, a in given.items():
        a = _np.ascontiguousarray(a)
        arrays[f"in_{name}_dram"] = a
        args.append(nc.dram_tensor(f"in_{name}_dram", a.shape, _mybir.dt.from_np(a.dtype), kind="ExternalInput").ap())
    for i, (shape, dtype) in enumerate(_OUTS):
        dt = _mybir.dt.from_np(_np.dtype(dtype))
        args.append(nc.dram_tensor(f"out_{i}_dram", shape, dt, kind="ExternalOutput").ap())
    build(nc, *args)
    r = _run(nc, [arrays], core_ids=[0])
    return r.results[0]["out_0_dram"]
```

```python
import concourse.bass as bass
from concourse import mybir
from contextlib import ExitStack

F32 = mybir.dt.float32
F32R = mybir.dt.float32r
BF16 = mybir.dt.bfloat16
I32 = mybir.dt.int32
U32 = mybir.dt.uint32
ALU = mybir.AluOpType
ACT = mybir.ActivationFunctionType
AX = mybir.AxisListType

P = 128
B, SEQ, D = 16, 256, 128
H, DH = 16, 64
G = H // 2
T = B * SEQ
NT = T // P
TB = SEQ // P
E, INTER, TOPK = 160, 64, 8
ROUTED_SCALE = 2.5
EPS = 1e-5
NSTEP = B * G
NBLK = T * TOPK // P + E
GB = 4
RING = 4
YR = 4
E_EARLY = 90
SEQ_BLK = SEQ * TOPK // P
COMBINE_FROM = 14
NGRP = NBLK // GB
CLEAR = NBLK // 8
BC = -(-NBLK // P)
TURNS = NGRP // RING
assert NGRP % RING == 0 and (TURNS - COMBINE_FROM) % YR == 0 and NT % YR == 0
assert E + 2 * SEQ_BLK <= NBLK // 2
assert RING * COMBINE_FROM >= (E + SEQ_BLK) // GB + RING
SCAT = [3, 4, 3, 3, 3]
SCAT_G = 6
assert sum(SCAT) == TB * TOPK


def build(nc, x, wqT, wkT, wv, wo, bo, rwT, ebias, wgd, wgsT, wdsT, out):
    slot_x = nc.dram_tensor("slot_x", [NBLK * P, D], F32).ap()
    block_y = nc.dram_tensor("block_y", [NBLK * P, D], F32).ap()

    with ExitStack() as ctx:
        def sb(name, shape, dt=F32, at=ctx):
            return at.enter_context(nc.sbuf_tensor(name, shape, dt))

        def sem(name):
            return ctx.enter_context(nc.semaphore(name))

        def wait(eng, s, value):
            if not isinstance(value, int) or value > 0:
                eng.wait_ge(s, value)

        held = {}

        def wait_apart(eng, s, value):
            if isinstance(value, int):
                wait(eng, s, value)
            else:
                eng.reg_mov(held[eng], value)
                eng.wait_ge(consts, 5)
                eng.wait_ge(s, held[eng])

        x_res = sb("x_res", [P, NT + TB, D])
        wE_res = sb("wE_res", [P, NT, TOPK])
        pos_u = sb("pos_u", [P, NT, TOPK], U32)
        ident = sb("ident", [P, P])
        ones_bf = sb("ones_bf", [P, P], BF16)
        tri = sb("tri", [P, P], BF16)
        mask_sum = sb("mask_sum", [P, E], BF16)
        blk_e = sb("blk_e", [P, BC])
        wgs_sb = sb("wgs_sb", [D, INTER])
        wds_sb = sb("wds_sb", [INTER, D])
        actx = ExitStack()
        with actx:
            def sa(name, shape, dt=F32):
                return sb(name, shape, dt, actx)

            xn2T_res = sa("xn2T_res", [P, T])
            rw_sb = sa("rw_sb", [D, E])
            eb_sb = sa("eb_sb", [P, TB, E])
            ones_row = sa("ones_row", [P, E])
            nb_old = sa("nb_old", [P, E])
            top_old = sa("top_old", [P, E])
            off_old = sa("off_old", [P, E])
            n_taken = sa("n_taken", [P, 1])
            cnt_i = sa("cnt_i", [P, E], I32)
            nb_i = sa("nb_i", [P, E], I32)
            nb_new = sa("nb_new", [P, E])
            taken = sa("taken", [P, E])
            first_new = sa("first_new", [P, E])
            off_new = sa("off_new", [P, E])
            shift = sa("shift", [P, E])
            moved = sa("moved", [P, E])
            beyond = sa("beyond", [P, TB, E])
            shifted = sa("shifted", [P, TB, E])
            offset = sa("offset", [P, TB, E])
            slot1 = sa("slot1", [P, TB, E])
            blk_num = sa("blk_num", [P, BC])
            blk_num_i = sa("blk_num_i", [P, BC], I32)
            le = sa("le", [P, BC, E])
            found = sa("found", [P, BC])
            free = sa("free", [P, BC])
            fix = sa("fix", [P, BC])
            rank_sb = sa("rank_sb", [P, TB + 1, E])
            st2 = sa("st2", [P, TB, 6])
            mv2 = sa("mv2", [P, TB, 2])
            ve2 = sa("ve2", [P, TB])
            rs2 = sa("rs2", [P, TB])
            half = sa("half", [P, TB])
            xn2 = sa("xn2", [P, TB, D])
            xn2_src = sa("xn2_src", [P, TB, D])
            xn2T = sa("xn2T", [D, SEQ])
            z_sb = sa("z_sb", [P, TB, E])
            ez_sb = sa("ez_sb", [P, TB, E])
            score = sa("score", [P, TB, E])
            repl = sa("repl", [P, TB, E])
            mask = sa("mask", [P, TB, E], BF16)
            part_sum = sa("part_sum", [P, E], BF16)
            top_s = sa("top_s", [P, TB, TOPK])
            top_w = sa("top_w", [P, TB, TOPK])
            top_i = sa("top_i", [P, TB, TOPK], U32)
            slot_m = sa("slot_m", [P, TB, E])
            slot8 = sa("slot8", [P, TB, TOPK])
            slot_u = sa("slot_u", [P, TB, TOPK], U32)
            e_of = sa("e_of", [P, TB, TOPK], U32)
            eq = sa("eq", [P, TB, TOPK, TOPK])
            eqw = sa("eqw", [P, TB, TOPK, TOPK])
            w_e = sa("w_e", [P, TB, TOPK])
            wsum = sa("wsum", [P, TB])
            wsc = sa("wsc", [P, TB])
            winv = sa("winv", [P, TB])
            m_hi = sa("m_hi", [D, H, D], F32R)
            m_lo = sa("m_lo", [D, H, D], F32R)
            wv_hi = sa("wv_hi", [D, H * DH], F32R)
            wv_lo = sa("wv_lo", [D, H * DH], F32R)
            wo_sb = sa("wo_sb", [P, G, D])
            bo_sb = sa("bo_sb", [P, TB, D])
            xn1 = sa("xn1", [P, TB, D])
            xnT_hi = sa("xnT_hi", [D, SEQ], F32R)
            xnT_lo = sa("xnT_lo", [D, SEQ], F32R)
            key_hi = sa("key_hi", [D, SEQ], F32R)
            key_lo = sa("key_lo", [D, SEQ], F32R)
            y_hi = sa("y_hi", [D, 2, 2, SEQ], F32R)
            y_lo = sa("y_lo", [D, 2, 2, SEQ], F32R)
            v_sb = sa("v_sb", [P, 2, TB, 2, P])
            p_sb = sa("p_sb", [P, 2, 2, TB, SEQ])
            pT_sb = sa("pT_sb", [P, 2, 2, TB, SEQ])
            oT_sb = sa("oT_sb", [P, 2, SEQ])
            negmax = sa("negmax", [P, 2, 2, TB])
            rowsum = sa("rowsum", [P, 2, 2, TB])
            rinv = sa("rinv", [P, 2, 2, TB])
            st1 = sa("st1", [P, TB, 6])
            mv1 = sa("mv1", [P, TB, 2])
            ve1 = sa("ve1", [P, TB])
            rs1 = sa("rs1", [P, TB])
            zero = sa("zero", [P, 8 * D])
            wqT_sb = sa("wqT_sb", [P, G, D])
            wkT_sb = sa("wkT_sb", [P, G, D])
            wv_sb = sa("wv_sb", [D, H * DH])

        yg = sb("yg", [P, YR, TOPK, D])
        blk_i = sb("blk_i", [P, NBLK], I32)
        xb = sb("xb", [P, RING, GB, D])
        xbT = sb("xbT", [D, 2, GB, P])
        y_b = sb("y_b", [P, 2, GB, D])
        acc = sb("acc", [P, YR, D])
        tok_idx = sb("tok_idx", [P, 2, YR, TOPK], U32)
        h_b = sb("h_b", [P, 2, GB // 2, P])
        w_b = sb("w_b", [P, RING, GB, INTER + D])
        hs = sb("hs", [INTER, 2, 4 * P])
        w_all = sb("w_all", [P, E, INTER + D])

        def bank(name, n=1, c=ctx):
            return c.enter_context(nc.psum_tensor(name, [P, n, 512], F32))

        psS = bank("psS", 2)
        psT = bank("psT", 2)
        psY = bank("psY")
        psVM = bank("psVM")
        psO = bank("psO")
        psA = bank("psA")

        consts = sem("consts")
        s = {}
        for name in """x0_in x_in wq_in wk_in wv_in c_in we_in zfill_a zfill_b yfill m_ps w_hi_ok w_lo_ok
                ln1_st ln1_ag ln1_ve ln1_rs ln1_xn xt_ps xt_hi xt_lo key_ok
                yq_ps yh_ok yl_ok v_ps v_ok s_ps nm_ok p_ok ri_ok pn_ok pna_ok t_ps pt0_ok pt1_ok o_ps ot_ok ao_ps
                xb_ok x1_ok ln2_st ln2_ag ln2_ve ln2_rs ln2_xn x2t_ps x2t_ok x2r_ok lg_ps z_ok ez_ok den_ok
                pr_ok top_ok rep_ok mask_ok rk_ps rk_cp sum_ok sm_ok s8_ok su_ok xs_ok eo_ok ti_ok eq_ok eqw_ok
                ws_ok wc_ok wi_ok wn_ok we_ok wr_ok scat
                b_ps b_dve b_pool tab_ok nbi_ok nbs_ok new_ok scan_ok fn_ok of_ok sh_ok by_ok bs_ok off_ok s1_ok mv_ok st_ok le_ok fr_ok fx_ok
                be_ok pu_ok
                w_cp xt2_ps xt2_ok g_ps h_ok y_ps y_ok
                idx_cp sh_ps hs_ok sho_ps shared_ok yw_ok ys_ok acc_ok""".split():
            s[name] = sem(name)
        ld = [sem(f"load{i}") for i in range(RING)]
        sty = [sem(f"store_y{i}") for i in range(2)]
        gat = [sem(f"gather{i}") for i in range(YR)]
        sto = [sem(f"store_out{i}") for i in range(YR)]

        def experts_of(eng, n):
            _, chosen = nc.values_load_multi_w_load_instructions(
                blk_i[0:1, bass.ds(n * GB, GB)], [eng.engine], min_val=0, max_val=E - 1,
                skip_runtime_bounds_check_because="the table holds min(expert, E - 1) of experts from 0")
            return chosen

        def live(b, g, lag, last=NSTEP):
            return not isinstance(b, int) or 0 <= G * b + g - lag < last

        def seq(b, lag):
            return not isinstance(b, int) or 0 <= b - lag < B

        def sequences(eng, body):
            body(0)
            body(1)
            body(2)
            body(3)
            with eng.Fori(4, B) as b:
                body(b)
            body(B)
            body(B + 1)
            body(B + 2)

        def heads(m, k):
            return m[:, k // 2 * 8 + k % 2:k // 2 * 8 + 8:2, :]

        def probs_transposed(eng, copy, h, g, u):
            wait(eng, s["t_ps"], 2 * u + h + 1)
            wait(eng, s["o_ps"], u - 1)
            copy(pT_sb[:, (g - 2) % 2, h].rearrange("p a t -> p (a t)"), psT[:, h, :]).then_inc(s[f"pt{h}_ok"], 1)

        block = ctx.enter_context(nc.Block())

        @block.sync
        def _(sp):
            xv = x.rearrange("b s d -> (b s) d").rearrange("(n p) d -> p n d", p=P)
            sp.dma_start(x_res[:, 0:TB, :], xv[:, 0:TB, :]).then_inc(s["x0_in"], 16)
            sp.dma_start(wqT_sb[:], wqT.rearrange("(g p) d -> p g d", p=P)).then_inc(s["wq_in"], 16)
            sp.dma_start(wkT_sb[:], wkT.rearrange("(g p) d -> p g d", p=P)).then_inc(s["wk_in"], 16)
            sp.dma_start(wv_sb[:], wv).then_inc(s["wv_in"], 16)
            sp.dma_start(x_res[:, TB:NT, :], xv[:, TB:NT, :]).then_inc(s["x_in"], 16)
            sp.dma_start(wo_sb[:], wo.rearrange("(g p) n -> p g n", p=P)).then_inc(s["c_in"], 16)
            sp.dma_start(rw_sb[:], rwT).then_inc(s["c_in"], 16)
            for i in range(TB):
                sp.dma_start(bo_sb[:, i, :], bo.partition_broadcast(P)).then_inc(s["c_in"], 16)
                sp.dma_start(eb_sb[:, i, :], ebias.partition_broadcast(P)).then_inc(s["c_in"], 16)
            sp.dma_start(wgs_sb[:], wgsT).then_inc(s["c_in"], 16)
            sp.dma_start(wds_sb[:], wdsT).then_inc(s["c_in"], 16)
            sp.wait_ge(consts, 5)
            def cleared(rows, c, n):
                v = rows.rearrange("(c p k) d -> p c (k d)", p=P, k=8)
                return v[:, bass.ds(c, n), :], zero[:, :].unsqueeze(1).broadcast_to([P, n, 8 * D])

            sp.dma_start(*cleared(slot_x, 0, CLEAR // 2)).then_inc(s["zfill_a"], 16)
            with sp.Fori(0, CLEAR // 4) as i:
                sp.wait_ge(s["s_ps"], 3 * i + 36)
                sp.dma_start(*cleared(slot_x, 2 * i + CLEAR // 2, 2)).then_inc(s["zfill_b"], 16)
            with sp.Fori(0, CLEAR // 2) as i:
                sp.wait_ge(s["s_ps"], 4 * i + 92)
                sp.dma_start(*cleared(block_y, 2 * i, 2)).then_inc(s["yfill"], 16)

            sp.wait_ge(s["w_lo_ok"], 5)
            sp.wait_ge(s["m_ps"], 1)
            sp.wait_ge(s["yfill"], 16 * (CLEAR // 2))
            with sp.Fori(0, (E - E_EARLY) // 10) as i:
                sp.wait_ge(s["s_ps"], 6 * i + 206)
                sp.dma_start(w_all[:, bass.ds(10 * i + E_EARLY, 10)], wgd[:, bass.ds(10 * i + E_EARLY, 10)]).then_inc(s["we_in"], 16)
            sp.wait_ge(s["ao_ps"], NSTEP)
            sp.wait_ge(s["x1_ok"], B)
            sp.wait_ge(s["xb_ok"], B)
            with sp.Fori(0, E_EARLY // 10) as i:
                sp.wait_ge(s["we_in"], 16 * i + 16 * ((E - E_EARLY) // 10))
                sp.dma_start(w_all[:, bass.ds(10 * i, 10)], wgd[:, bass.ds(10 * i, 10)]).then_inc(s["we_in"], 16)
            sp.wait_ge(s["wr_ok"], B)
            sp.wait_ge(s["be_ok"], B)
            sp.wait_ge(s["x2r_ok"], B)
            sp.wait_ge(s["scat"], 16 * NT * TOPK)
            xv = slot_x.rearrange("(n b p) d -> n p b d", b=GB, p=P)

            def load_group(it, r, first):
                n = RING * it + r
                if not first:
                    sp.wait_ge(s["xt2_ps"], n - RING + 1)
                sp.dma_start(xb[:, r], xv[bass.ds(n, 1)].rearrange("o p b d -> (o p) b d")).then_inc(ld[r], 16)

            ov = out.rearrange("b s d -> (b s) d").rearrange("(n p) d -> n p d", p=P)

            def store_out(n, r):
                sp.wait_ge(s["acc_ok"], n + 1)
                sp.dma_start(ov[bass.ds(n, 1)].rearrange("o p d -> (o p) d"), acc[:, r, :]).then_inc(sto[r], 16)

            for r in range(RING):
                load_group(0, r, True)
            with sp.Fori(1, COMBINE_FROM) as it:
                for r in range(RING):
                    load_group(it, r, False)

            def turns(q, first):
                for k in range(YR):
                    for r in range(RING):
                        load_group(YR * q + (COMBINE_FROM + k), r, False)
                    if not first or k > 0:
                        store_out(YR * q + (k - 1), (k - 1) % YR)

            turns(0, True)
            with sp.Fori(1, (TURNS - COMBINE_FROM) // YR) as q:
                turns(q, False)
            store_out(TURNS - COMBINE_FROM - 1, YR - 1)
            with sp.Fori((TURNS - COMBINE_FROM) // YR, NT // YR) as q:
                for k in range(YR):
                    store_out(YR * q + k, k)
            for r in range(YR):
                sp.wait_ge(sto[r], 16 * (NT // YR))

        @block.tensor
        def _(pe):
            def split_product(dst, wsl, xsl, last):
                for n, (a, c) in enumerate(((0, 0), (0, 1), (1, 0))):
                    m = pe.matmul(dst, wsl[a], xsl[c], start=(n == 0), stop=(n == 2))
                if last is not None:
                    m.then_inc(last, 1)

            def body(b):
                for g in range(G):
                    step = G * b + g
                    if live(b, g, 1):
                        u = step - 1
                        wait(pe, s["yh_ok"], u + 1)
                        wait(pe, s["yl_ok"], u + 1)
                        wait(pe, s["key_ok"], 2 * b if g == 0 else 2 * b + 2)
                        for h in range(2):
                            wait(pe, s["p_ok"], 4 * u - 2 + 2 * h)
                            for qt in range(TB):
                                q = (slice(None), (g - 1) % 2, h, slice(qt * P, (qt + 1) * P))
                                split_product(psS[:, h, qt * SEQ:(qt + 1) * SEQ], (y_hi[q], y_lo[q]), (key_hi[:], key_lo[:]),
                                              s["s_ps"] if qt == TB - 1 else None)
                    if live(b, g, 0):
                        if g == 0:
                            wait(pe, s["xt_hi"], b + 1)
                            wait(pe, s["xt_lo"], b + 1)
                        wait(pe, s["yl_ok"], step)
                        for h in range(2):
                            split_product(psY[:, 0, h * SEQ:(h + 1) * SEQ], (m_hi[:, 2 * g + h, :], m_lo[:, 2 * g + h, :]),
                                          (xnT_hi[:], xnT_lo[:]), s["yq_ps"] if h == 1 else None)
                    if g == G - 1 and live(b, g, 0):
                        values_read(b, g)
                        if seq(b, 1):
                            wait(pe, s["z_ok"], b)
                        input_transpose(b + 1)
                    if live(b, g, 3):
                        u = step - 3
                        wait(pe, s["pt0_ok"], u + 1)
                        wait(pe, s["pt1_ok"], u + 1)
                        wait(pe, s["ot_ok"], u)
                        for kt in range(TB):
                            for h in range(2):
                                m = pe.matmul(psO[h * DH:(h + 1) * DH, 0, 0:SEQ],
                                              v_sb[:, (g - 3) // 2 % 2, kt, (g - 3) % 2, h * DH:(h + 1) * DH],
                                              pT_sb[:, (g - 3) % 2, h, kt, :], start=(kt == 0), stop=(kt == TB - 1))
                        m.then_inc(s["o_ps"], 1)
                    if g % 2 == 0 and live(b, g, 0):
                        values(b, g)
                    if live(b, g, 2):
                        u = step - 2
                        for h in range(2):
                            wait(pe, s["pn_ok"], 3 * u + 2 + h)
                            if h == 1:
                                wait(pe, s["pna_ok"], u + 1)
                            wait(pe, s[f"pt{h}_ok"], u)
                            for qt in range(TB):
                                for kt in range(TB):
                                    m = pe.transpose(psT[:, h, kt * SEQ + qt * P:kt * SEQ + (qt + 1) * P],
                                                     p_sb[:, (g - 2) % 2, h, qt, kt * P:(kt + 1) * P], ident[:])
                            m.then_inc(s["t_ps"], 1)
                    if live(b, g, 4):
                        u = step - 4
                        wait(pe, s["ot_ok"], u + 1)
                        gp = (g - 4) % G
                        if gp == 0:
                            wait(pe, s["x1_ok"], b)
                        for i in range(TB):
                            m = pe.matmul(psA[:, 0, i * P:(i + 1) * P], oT_sb[:, (g - 4) % 2, i * P:(i + 1) * P],
                                          wo_sb[:, gp, :], start=(gp == 0 and i == 0), stop=(gp == G - 1),
                                          skip_group_check=True)
                        m.then_inc(s["ao_ps"], 1)
                    if g == 1 and seq(b, 2):
                        values_read(b, g)
                        wait(pe, s["mask_ok"], b - 1)
                        wait(pe, s["sum_ok"], b - 1)
                        ranks(b)
                    if g == 5 and seq(b, 1):
                        values_read(b, g)
                        wait(pe, s["ln2_xn"], TB * b)
                        for i in range(TB):
                            m = pe.transpose(psVM[:, 0, i * P:(i + 1) * P], xn2[:, i, :], ident[:])
                        m.then_inc(s["x2t_ps"], 1)
                    if g == 6 and seq(b, 1):
                        values_read(b, g)
                        wait(pe, s["x2t_ok"], b)
                        for i in range(TB):
                            m = pe.matmul(psVM[:, 0, i * E:(i + 1) * E], xn2T[:, i * P:(i + 1) * P], rw_sb[:],
                                          start=True, stop=True)
                        m.then_inc(s["lg_ps"], 1)

            def values(b, g):
                wait(pe, s["v_ok"], G // 2 * b + g // 2)
                if g == 2 and seq(b, 2):
                    wait(pe, s["rk_cp"], b - 1)
                if g == 6 and seq(b, 1):
                    wait(pe, s["x2t_ok"], b)
                for i in range(TB):
                    r = slice(i * P, (i + 1) * P)
                    c = slice(g * P, (g + 2) * P)
                    split_product(psVM[:, 0, i * 2 * P:(i + 1) * 2 * P], (xnT_hi[:, r], xnT_lo[:, r]),
                                  (wv_hi[:, c], wv_lo[:, c]), s["v_ps"] if i == TB - 1 else None)

            def values_read(b, g):
                if live(b, 0, 0):
                    wait(pe, s["v_ok"], G // 2 * b + g // 2 + 1)

            def ranks(b):
                for i in range(TB):
                    o = psVM[:, 0, i * E:(i + 1) * E]
                    pe.matmul(o, tri[:], mask[:, i, :], start=True, stop=False)
                    for j in range(i):
                        pe.matmul(o, ones_bf[:], mask[:, j, :], start=False, stop=False)
                    pe.matmul(o, ones_bf[:], mask_sum[:], start=False, stop=True)
                o = psVM[:, 0, TB * E:(TB + 1) * E]
                pe.matmul(o, ones_bf[:], mask_sum[:], start=True, stop=False)
                for j in range(TB):
                    m = pe.matmul(o, ones_bf[:], mask[:, j, :], start=False, stop=(j == TB - 1))
                m.then_inc(s["rk_ps"], 1)

            def input_transpose(b):
                wait(pe, s["ln1_xn"], TB * (b + 1))
                for i in range(TB):
                    m = pe.transpose(psVM[:, 0, i * P:(i + 1) * P], xn1[:, i, :], ident[:])
                m.then_inc(s["xt_ps"], 1)

            pe.wait_ge(consts, 5)
            input_transpose(0)
            pe.wait_ge(s["wq_in"], 16)
            pe.wait_ge(s["wk_in"], 16)
            for g in range(G):
                for h in range(2):
                    r = slice(h * DH, (h + 1) * DH)
                    m = pe.matmul((psS, psT)[g // 4][:, h, g % 4 * D:(g % 4 + 1) * D], wqT_sb[r, g, :], wkT_sb[r, g, :],
                                  start=True, stop=True)
            m.then_inc(s["m_ps"], 1)
            pe.wait_ge(s["w_hi_ok"], 5)
            pe.wait_ge(s["w_lo_ok"], 5)
            pe.wait_ge(s["c_in"], 16 * (4 + 2 * TB))
            sequences(pe, body)

            pe.wait_ge(s["x2r_ok"], B)
            pe.wait_ge(s["ot_ok"], NSTEP)
            pe.wait_ge(s["x1_ok"], B)
            pe.wait_ge(s["pt0_ok"], NSTEP)
            pe.wait_ge(s["pt1_ok"], NSTEP)

            def shared_hidden(n, r, first):
                if not first:
                    pe.wait_ge(s["hs_ok"], n - 1)
                pe.matmul((psO, psA)[r][0:INTER, 0, :], wgs_sb[:], xn2T_res[:, bass.ds(n * 4 * P, 4 * P)],
                          start=True, stop=True).then_inc(s["sh_ps"], 1)

            def shared_out(n, r, first):
                pe.wait_ge(s["hs_ok"], n + 1)
                if not first:
                    pe.wait_ge(s["shared_ok"], n - 1)
                for i in range(4):
                    m = pe.matmul(psT[:, r, i * P:(i + 1) * P], hs[:, r, i * P:(i + 1) * P], wds_sb[:], start=True, stop=True)
                m.then_inc(s["sho_ps"], 1)

            shared_hidden(0, 0, True)
            shared_hidden(1, 1, True)
            shared_out(0, 0, True)
            shared_hidden(2, 0, False)
            shared_out(1, 1, True)
            shared_hidden(3, 1, False)
            with pe.Fori(2, NT // 8) as it:
                for r in range(2):
                    shared_out(2 * it + (r - 2), r, False)
                    shared_hidden(2 * it + r, r, False)
            for r in range(2):
                shared_out(NT // 4 - 2 + r, r, False)

            pe.wait_ge(s["be_ok"], B)
            pe.wait_ge(s["z_ok"], B)
            for c in range(BC):
                n = min(P, NBLK - c * P)
                m = pe.matmul(psY[:, 0, c * P:c * P + n], blk_e[:, c:c + 1].broadcast_to([P, P]), ident[:, 0:n],
                              start=True, stop=True)
            m.then_inc(s["b_ps"], 1)
            pe.wait_ge(s["shared_ok"], NT // 4)
            pe.wait_ge(s["tab_ok"], 1)

            def transposes(it, r, n):
                par = r % 2
                pe.wait_ge(ld[r], 16 * (it + 1))
                wait(pe, s["xt2_ok"], n - 1)
                for i in range(GB):
                    m = pe.transpose(psT[:, par, i * P:(i + 1) * P], xb[:, r, i, :], ident[:])
                m.then_inc(s["xt2_ps"], 1)

            def gates(r, n):
                par = r % 2
                pe.wait_ge(s["xt2_ok"], n + 1)
                pe.wait_ge(s["w_cp"], n + 1)
                wait(pe, s["h_ok"], n - 1)
                for i in range(GB):
                    half = slice(i % 2 * INTER, (i % 2 + 1) * INTER)
                    m = pe.matmul(psS[half, par, i // 2 * P:(i // 2 + 1) * P], w_b[:, r, i, 0:INTER], xbT[:, par, i, :],
                                  start=True, stop=True)
                m.then_inc(s["g_ps"], 1)

            def downs(r, n):
                par = r % 2
                ps = ((psY, psVM), (psO, psA))[par]
                pe.wait_ge(s["h_ok"], n + 1)
                wait(pe, s["y_ok"], n - 1)
                for i in range(GB):
                    half = slice(i % 2 * INTER, (i % 2 + 1) * INTER)
                    m = pe.matmul(ps[i % 2][:, 0, i // 2 * P:(i // 2 + 1) * P], h_b[half, par, i // 2, :], w_b[half, r, i, INTER:],
                                  start=True, stop=True)
                m.then_inc(s["y_ps"], 1)

            def experts(it, first):
                for r in range(RING):
                    n = RING * it + r
                    transposes(it, r, n)
                    if not (first and r < 1):
                        gates((r - 1) % RING, n - 1)
                    if not (first and r < 2):
                        downs((r - 2) % RING, n - 2)

            experts(0, True)
            with pe.Fori(1, NGRP // RING) as it:
                experts(it, False)
            gates(RING - 1, NGRP - 1)
            downs(RING - 2, NGRP - 2)
            downs(RING - 1, NGRP - 1)

        @block.scalar
        def _(act):
            act.wait_ge(s["wv_in"], 16)
            act.copy(wv_hi[:], wv_sb[:]).then_inc(s["w_hi_ok"], 1)
            act.wait_ge(s["m_ps"], 1)
            for k in range(4):
                act.activation(heads(m_hi, k), (psS, psT)[k // 2][:, k % 2, :].rearrange("p (g d) -> p g d", g=4),
                               ACT.Copy, scale=DH ** -0.5).then_inc(s["w_hi_ok"], 1)

            def body(b):
                for g in range(G):
                    step = G * b + g
                    if live(b, g, 0):
                        wait(act, s["yq_ps"], step + 1)
                        wait(act, s["s_ps"], 2 * (step - 1))
                        act.copy(y_hi[:, g % 2].rearrange("p a t -> p (a t)"), psY[:, 0, :]).then_inc(s["yh_ok"], 1)
                    if g == 0 and live(b, g, 0):
                        wait(act, s["s_ps"], 2 * step)
                        wait(act, s["xt_hi"], b + 1)
                        wait(act, s["xt_lo"], b + 1)
                        act.copy(key_hi[:], xnT_hi[:].bitcast(F32)).then_inc(s["key_ok"], 1)
                        act.copy(key_lo[:], xnT_lo[:].bitcast(F32)).then_inc(s["key_ok"], 1)
                    if live(b, g, 1):
                        u = step - 1
                        wait(act, s["t_ps"], 2 * u - 2)
                        wait(act, s["ri_ok"], u - 1)
                        for h in range(2):
                            wait(act, s["nm_ok"], 2 * u + h + 1)
                            for qt in range(TB):
                                act.activation(p_sb[:, (g - 1) % 2, h, qt, :], psS[:, h, qt * SEQ:(qt + 1) * SEQ], ACT.Exp,
                                               bias=negmax[:, (g - 1) % 2, h, qt:qt + 1], scale=1.0,
                                               accum_out=rowsum[:, (g - 1) % 2, h, qt:qt + 1]).then_inc(s["p_ok"], 1)
                    if g % 2 == 0 and live(b, g, 0):
                        wait(act, s["v_ps"], G // 2 * b + g // 2 + 1)
                        wait(act, s["o_ps"], step - 2)
                        act.copy(v_sb[:, g // 2 % 2].rearrange("p t a d -> p (t a d)"), psVM[:, 0, :]).then_inc(s["v_ok"], 1)
                    if live(b, g, 2):
                        for h in range(2):
                            probs_transposed(act, act.copy, h, g, step - 2)
                    if live(b, g, 1):
                        u = step - 1
                        wait(act, s["ri_ok"], u + 1)
                        pq = p_sb[:, (g - 1) % 2, 1, 1, :]
                        act.activation(pq, pq, ACT.Copy, scale=rinv[:, (g - 1) % 2, 1, 1:2]).then_inc(s["pna_ok"], 1)
                    if g == 7 and seq(b, 1):
                        wait(act, s["z_ok"], b)
                        wait(act, s["den_ok"], b - 1)
                        act.activation(ez_sb[:], z_sb[:], ACT.Exp, scale=-1.0).then_inc(s["ez_ok"], 1)
                        wait(act, s["x2t_ok"], b)
                        act.copy(xn2T_res[:, bass.ds((b - 1) * SEQ, SEQ)], xn2T[:]).then_inc(s["x2r_ok"], 1)

            sequences(act, body)

            act.wait_ge(s["x2r_ok"], B)

            def shared(n, r, first):
                act.wait_ge(s["sh_ps"], n + 1)
                if not first:
                    act.wait_ge(s["sho_ps"], n - 1)
                act.activation(hs[:, r, :], (psO, psA)[r][0:INTER, 0, :], ACT.Silu).then_inc(s["hs_ok"], 1)

            for n in range(2):
                shared(n, n, True)
            with act.Fori(1, NT // 8) as it:
                for r in range(2):
                    shared(2 * it + r, r, False)

            act.wait_ge(s["sho_ps"], NT // 4)
            def evac(r, n):
                par = r % 2
                act.wait_ge(s["xt2_ps"], n + 1)
                wait(act, s["g_ps"], n - 1)
                act.copy(xbT[:, par].rearrange("p a t -> p (a t)"), psT[:, par, :]).then_inc(s["xt2_ok"], 1)

            def silu(r, n):
                par = r % 2
                act.wait_ge(s["g_ps"], n + 1)
                wait(act, s["y_ps"], n - 1)
                act.activation(h_b[:, par].rearrange("p k t -> p (k t)"), psS[:, par, 0:GB // 2 * P],
                               ACT.Silu).then_inc(s["h_ok"], 1)

            def outputs(r, n, first):
                par = r % 2
                act.wait_ge(s["y_ps"], n + 1)
                if not first:
                    act.wait_ge(sty[par], 8 * (n - par))
                for k in range(2):
                    m = act.copy(y_b[:, par, k::2, :], ((psY, psVM), (psO, psA))[par][k][:, 0, 0:GB // 2 * P].rearrange("p (a d) -> p a d", d=D))
                m.then_inc(s["y_ok"], 1)

            act.wait_ge(s["yfill"], 16 * (CLEAR // 2))

            def store_y(r, n):
                par = r % 2
                act.wait_ge(s["y_ok"], n + 1)
                act.dma_start(block_y.rearrange("(n b p) d -> n p b d", b=GB, p=P)[bass.ds(n, 1)].rearrange("o p b d -> (o p) b d"),
                              y_b[:, par]).then_inc(sty[par], 16)

            def experts(it, first):
                for r in range(RING):
                    n = RING * it + r
                    evac(r, n)
                    if not (first and r < 3):
                        store_y((r - 3) % RING, n - 3)
                    if not (first and r < 1):
                        silu((r - 1) % RING, n - 1)
                    if not (first and r < 2):
                        outputs((r - 2) % RING, n - 2, first)

            experts(0, True)
            with act.Fori(1, NGRP // RING) as it:
                experts(it, False)
            silu(RING - 1, NGRP - 1)
            store_y(RING - 3, NGRP - 3)
            for k in (2, 1):
                outputs(RING - k, NGRP - k, False)
                store_y(RING - k, NGRP - k)
            for par in range(2):
                act.wait_ge(sty[par], 8 * NGRP)

        @block.gpsimd
        def _(pool):
            held[pool] = pool.alloc_register("pool_wait")
            pool.memset(ident[:], 0.0).then_inc(s["b_pool"], 1)
            pool.wait_ge(s["b_pool"], 1)
            pool.affine_select(out=ident[:], in_=ident[:], compare_op=ALU.not_equal, fill=1.0, base=0,
                               pattern=[[-1, P]], channel_multiplier=1).then_inc(consts, 1)
            pool.memset(half[:], -0.5).then_inc(consts, 1)
            pool.memset(zero[:], 0.0).then_inc(consts, 1)
            pool.memset(ones_bf[:], 1.0).then_inc(consts, 1)
            pool.memset(x_res[:, NT:NT + TB, :], 0.0).then_inc(consts, 1)
            pool.wait_ge(consts, 5)
            pool.wait_ge(s["ln1_ve"], 1)
            pool.tensor_tensor(rs1[:], ve1[:], half[:], ALU.pow).then_inc(s["ln1_rs"], 1)
            pool.memset(tri[:], 0.0).then_inc(s["b_pool"], 1)
            for t in (nb_old, top_old, off_old, n_taken):
                pool.memset(t[:], 0.0).then_inc(s["b_pool"], 1)
            pool.memset(blk_e[:], float(E)).then_inc(s["b_pool"], 1)
            pool.memset(ones_row[:], 1.0).then_inc(s["b_pool"], 1)
            pool.memset(mask_sum[:], 0.0).then_inc(s["sum_ok"], 1)
            pool.wait_ge(s["b_pool"], 8)
            pool.affine_select(out=tri[:], in_=tri[:], compare_op=ALU.is_ge, fill=1.0, base=0,
                               pattern=[[-1, P]], channel_multiplier=1).then_inc(s["b_pool"], 1)
            pool.iota(blk_num_i[:], pattern=[[P, BC]], base=0, channel_multiplier=1).then_inc(s["b_pool"], 1)

            def body(b):
                for g in range(G):
                    step = G * b + g
                    if g == 4 and seq(b, 2):
                        wait_apart(pool, s["mask_ok"], b - 1)
                        wait_apart(pool, s["scat"], 16 * TB * TOPK * (b - 2))
                        pool.tensor_scalar(xn2_src[:], xn2[:], 1.0, 1.0, ALU.mult, ALU.mult).then_inc(s["xs_ok"], 1)
                    if g == 4 and seq(b, 1):
                        wait(pool, s["ln2_ve"], b)
                        pool.tensor_tensor(rs2[:], ve2[:], half[:], ALU.pow).then_inc(s["ln2_rs"], 1)
                    if g == 5 and (not isinstance(b, int) or b < B):
                        wait(pool, s["ln1_ve"], b + 2)
                        pool.tensor_tensor(rs1[:], ve1[:], half[:], ALU.pow).then_inc(s["ln1_rs"], 1)
                    if live(b, g, 1):
                        u = step - 1
                        wait_apart(pool, s["ri_ok"], u + 1)
                        for k in range(3):
                            pq = p_sb[:, (g - 1) % 2, k // 2, k % 2, :]
                            pool.tensor_scalar(pq, pq, rinv[:, (g - 1) % 2, k // 2, k % 2:k % 2 + 1], 1.0, ALU.mult,
                                               ALU.mult).then_inc(s["pn_ok"], 1)
                    if g == 2 and live(b, g, 0):
                        if isinstance(b, int) and b == 0:
                            pool.wait_ge(s["c_in"], 16 * (4 + 2 * TB))
                        wait(pool, s["ln1_xn"], TB * (b + 1))
                        xr = x_res[:, bass.ds(b * TB, TB), :]
                        pool.tensor_tensor(xr, xr, bo_sb[:], ALU.add).then_inc(s["xb_ok"], 1)
                    scatter(b, g)

            def scatter(b, g):
                k = (g - SCAT_G) % G
                if k < len(SCAT) and seq(b, 2 if g >= SCAT_G else 3):
                    if k == 0:
                        wait_apart(pool, s["su_ok"], b - 1)
                        wait_apart(pool, s["xs_ok"], b - 1)
                        pool.wait_ge(s["zfill_a"], 16)
                        if not isinstance(b, int) or b > 3:
                            pool.wait_ge(s["zfill_b"], 16 * (CLEAR // 4))
                    k0 = sum(SCAT[:k])
                    for n in range(k0, k0 + SCAT[k]):
                        i, j = n // TOPK, n % TOPK
                        pool.indirect_dma_start(slot_x, bass.IndirectOffsetOnAxis(ap=slot_u[:, i, j:j + 1], axis=0),
                                                xn2_src[:, i, :], None).then_inc(s["scat"], 16)

            sequences(pool, body)

            pool.wait_ge(s["wr_ok"], B)
            pool.wait_ge(s["pu_ok"], B)
            pool.wait_ge(s["scat"], 16 * NT * TOPK)

            def slots_of(n, par):
                pool.tensor_copy(tok_idx[:, par], pos_u[:, bass.ds(n, YR), :]).then_inc(s["idx_cp"], 1)

            def gather(n, b, par, r):
                if not isinstance(n, int) or n >= YR:
                    wait_apart(pool, s["ys_ok"], n - YR + 1)
                if r % TB == 0:
                    for k in range(2):
                        wait_apart(pool, sty[k], 8 * SEQ_BLK // GB * b + 8 * (E + SEQ_BLK) // GB)
                for k in range(TOPK):
                    pool.indirect_dma_start(yg[:, r, k, :], None, block_y,
                                            bass.IndirectOffsetOnAxis(ap=tok_idx[:, par, r, k:k + 1], axis=0)).then_inc(gat[r], 16)

            def gathers(q, par, last):
                for r in range(YR):
                    gather(YR * q + r, YR // TB * q + r // TB, par, r)
                    if r == YR - 1 and not last:
                        slots_of(YR * q + YR, 1 - par)
                if not last:
                    wait_apart(pool, s["idx_cp"], q + 2)

            slots_of(0, 0)
            pool.wait_ge(s["idx_cp"], 1)
            gathers(0, 0, False)
            gathers(1, 1, False)
            with pool.Fori(1, NT // YR // 2 - 1) as i:
                for par in range(2):
                    gathers(2 * i + par, par, False)
            gathers(NT // YR - 2, 0, False)
            gathers(NT // YR - 1, 1, True)

        @block.vector
        def _(dve):
            def ln_stats(b, which, st, mv, ve):
                if which == "ln2":
                    wait_apart(dve, s["x1_ok"], b + 1)
                for i in range(TB):
                    src = x_res[:, bass.ds(b * TB + i, 1), :].rearrange("p o d -> p (o d)")
                    m = dve.bn_stats(st[:, i, :], src)
                m.then_inc(s[which + "_st"], 1)
                wait_apart(dve, s[which + "_st"], b + 1)
                for i in range(TB):
                    m = dve.bn_aggr(mv[:, i, :], st[:, i, :])
                m.then_inc(s[which + "_ag"], 1)
                wait(dve, s[which + "_ag"], b + 1)
                dve.tensor_scalar(ve[:], mv[:, :, 1], EPS, None, ALU.add).then_inc(s[which + "_ve"], 1)

            def ln_apply(b, which, dst, mv, rs):
                wait(dve, s[which + "_rs"], b + 1)
                for i in range(TB):
                    src = x_res[:, bass.ds(b * TB + i, 1), :].rearrange("p o d -> p (o d)")
                    dve.tensor_scalar(dst[:, i, :], src, mv[:, i, 0:1], rs[:, i:i + 1], ALU.subtract,
                                      ALU.mult).then_inc(s[which + "_xn"], 1)

            def input_split(b):
                wait(dve, s["xt_ps"], b + 1)
                wait(dve, s["v_ps"], G // 2 * b)
                wait(dve, s["yq_ps"], G * b)
                wait(dve, s["key_ok"], 2 * b)
                dve.tensor_copy(xnT_hi[:], psVM[:, 0, 0:SEQ]).then_inc(s["xt_hi"], 1)
                wait(dve, s["xt_hi"], b + 1)
                dve.tensor_tensor(xnT_lo[:], psVM[:, 0, 0:SEQ], xnT_hi[:].bitcast(F32), ALU.subtract).then_inc(s["xt_lo"], 1)

            held[dve] = dve.alloc_register("dve_wait")
            dve.wait_ge(s["x0_in"], 16)
            ln_stats(0, "ln1", st1, mv1, ve1)
            ln_apply(0, "ln1", xn1, mv1, rs1)
            input_split(0)
            dve.wait_ge(s["w_hi_ok"], 1)
            dve.tensor_tensor(wv_lo[:], wv_sb[:], wv_hi[:].bitcast(F32), ALU.subtract).then_inc(s["w_lo_ok"], 1)
            for k in range(4):
                dve.wait_ge(s["w_hi_ok"], k + 2)
                dve.scalar_tensor_tensor(out=heads(m_lo, k), in0=(psS, psT)[k // 2][:, k % 2, :].rearrange("p (g d) -> p g d", g=4),
                                         scalar=DH ** -0.5, in1=heads(m_hi, k).bitcast(F32), op0=ALU.mult,
                                         op1=ALU.subtract).then_inc(s["w_lo_ok"], 1)
            dve.wait_ge(s["x_in"], 16)
            dve.wait_ge(consts, 5)
            dve.wait_ge(s["b_pool"], 10)
            dve.tensor_copy(blk_num[:], blk_num_i[:]).then_inc(s["b_dve"], 1)
            dve.wait_ge(s["b_dve"], 1)
            dve.wait_ge(s["c_in"], 16 * (4 + 2 * TB))

            def choose(b, inverse_sums):
                n = b - 1
                wait(dve, s["ez_ok"], n)
                dve.tensor_scalar(score[:], ez_sb[:], -1.0, -1.0, ALU.mult, ALU.add).then_inc(s["den_ok"], 1)
                wait_apart(dve, s["den_ok"], n)
                for i in range(TB):
                    m = dve.max(top_s[:, i, :], score[:, i, :])
                m.then_inc(s["top_ok"], 1)
                inverse_sums()
                wait_apart(dve, s["top_ok"], n)
                for i in range(TB):
                    m = dve.match_replace(repl[:, i, :], top_s[:, i, :], score[:, i, :], 0.0)
                m.then_inc(s["rep_ok"], 1)
                wait(dve, s["rep_ok"], n)
                dve.tensor_tensor(mask[:], score[:], repl[:], ALU.not_equal).then_inc(s["mask_ok"], 1)

            def slots(b, inverse_sums):
                n = b - 1
                last = TB * E
                wait(dve, s["rk_ps"], n)
                wait(dve, s["s1_ok"], n - 1)
                dve.tensor_copy(rank_sb[:].rearrange("p i e -> p (i e)"), psVM[:, 0, 0:last + E]).then_inc(s["rk_cp"], 1)
                inverse_sums()
                wait(dve, s["rk_cp"], n)
                dve.tensor_scalar(cnt_i[:], rank_sb[:, TB, :], float(P - 1), None, ALU.add).then_inc(s["nbi_ok"], 1)
                wait(dve, s["st_ok"], 4 * (n - 1))
                dve.tensor_tensor(beyond[:], rank_sb[:, 0:TB, :], row(top_old), ALU.is_ge).then_inc(s["by_ok"], 1)
                wait(dve, s["nbi_ok"], n)
                dve.tensor_scalar(nb_i[:], cnt_i[:], P.bit_length() - 1, None, ALU.logical_shift_right).then_inc(s["nbs_ok"], 1)
                part_counts(n)
                wait(dve, s["nbs_ok"], n)
                dve.tensor_tensor(nb_new[:], nb_i[:], nb_old[:], ALU.subtract).then_inc(s["new_ok"], 1)
                wait(dve, s["new_ok"], n)
                dve.tensor_tensor_scan(taken[:], ones_row[:], nb_new[:], n_taken[:, 0:1], ALU.mult, ALU.add).then_inc(s["scan_ok"], 1)

            def row(t):
                return t[:].unsqueeze(1).broadcast_to([P, TB, E])

            def offsets(b, inverse_sums):
                n = b - 1
                wait(dve, s["scan_ok"], n)
                dve.tensor_tensor(first_new[:], taken[:], nb_new[:], ALU.subtract).then_inc(s["fn_ok"], 1)
                wait(dve, s["fn_ok"], n)
                dve.tensor_tensor(off_new[:], first_new[:], nb_old[:], ALU.subtract).then_inc(s["of_ok"], 1)
                wait(dve, s["of_ok"], n)
                dve.scalar_tensor_tensor(out=shift[:], in0=off_new[:], scalar=float(P), in1=off_old[:], op0=ALU.mult,
                                         op1=ALU.subtract).then_inc(s["sh_ok"], 1)
                inverse_sums()
                wait(dve, s["sh_ok"], n)
                wait(dve, s["by_ok"], n)
                dve.tensor_tensor(shifted[:], beyond[:], row(shift), ALU.mult).then_inc(s["bs_ok"], 1)
                dve.scalar_tensor_tensor(out=moved[:], in0=nb_new[:], scalar=0.5, in1=shift[:], op0=ALU.is_gt,
                                         op1=ALU.mult).then_inc(s["mv_ok"], 1)

            def slot_numbers(b, inverse_sums):
                n = b - 1
                wait(dve, s["bs_ok"], n)
                dve.tensor_tensor(offset[:], shifted[:], row(off_old), ALU.add).then_inc(s["off_ok"], 1)
                wait(dve, s["off_ok"], n)
                dve.scalar_tensor_tensor(out=slot1[:], in0=rank_sb[:, 0:TB, :], scalar=1.0, in1=offset[:], op0=ALU.add,
                                         op1=ALU.add).then_inc(s["s1_ok"], 1)
                inverse_sums()

            def new_state(b, inverse_sums):
                n = b - 1
                wait(dve, s["s1_ok"], n)
                dve.tensor_tensor(slot_m[:], slot1[:], mask[:], ALU.mult).then_inc(s["sm_ok"], 1)
                wait(dve, s["mv_ok"], n)
                dve.tensor_tensor(off_old[:], off_old[:], moved[:], ALU.add).then_inc(s["st_ok"], 1)
                dve.tensor_copy(nb_old[:], nb_i[:]).then_inc(s["st_ok"], 1)
                dve.tensor_scalar(top_old[:], nb_i[:], float(P), None, ALU.mult).then_inc(s["st_ok"], 1)
                dve.tensor_copy(n_taken[:], taken[:, E - 1:E]).then_inc(s["st_ok"], 1)
                inverse_sums()

            def chosen_slots(b, inverse_sums):
                n = b - 1
                wait_apart(dve, s["sm_ok"], n)
                for i in range(TB):
                    m = dve.max(slot8[:, i, :], slot_m[:, i, :])
                m.then_inc(s["s8_ok"], 1)
                wait(dve, s["s8_ok"], n)
                wait(dve, s["scat"], 16 * TB * TOPK * (b - 2))
                dve.tensor_scalar(slot_u[:], slot8[:], -1.0, None, ALU.add).then_inc(s["su_ok"], 1)
                inverse_sums()
                for i in range(TB):
                    m = dve.max_index(e_of[:, i, :], slot8[:, i, :], slot_m[:, i, :])
                m.then_inc(s["eo_ok"], 1)
                wait(dve, s["su_ok"], n)
                dve.tensor_copy(pos_u[:, bass.ds((b - 2) * TB, TB), :], slot_u[:]).then_inc(s["pu_ok"], 1)

            def part_counts(n):
                wait(dve, s["sum_ok"], n)
                dve.tensor_tensor(part_sum[:], mask_sum[:], mask[:, 0, :], ALU.add).then_inc(s["ws_ok"], 1)
                wait(dve, s["ws_ok"], n)
                dve.tensor_tensor(mask_sum[:], part_sum[:], mask[:, 1, :], ALU.add).then_inc(s["sum_ok"], 1)

            def blocks(b):
                n = b - 1
                for c in range(BC):
                    m = dve.tensor_scalar(le[:, c, :], taken[:], blk_num[:, c:c + 1], None, ALU.is_le, ALU.add,
                                          accum_out=found[:, c:c + 1])
                m.then_inc(s["le_ok"], 1)
                wait(dve, s["be_ok"], n - 1)
                dve.tensor_scalar(free[:], blk_e[:], E - 0.5, None, ALU.is_gt).then_inc(s["fr_ok"], 1)
                wait(dve, s["fr_ok"], n)
                wait(dve, s["le_ok"], n)
                dve.scalar_tensor_tensor(out=fix[:], in0=found[:], scalar=-float(E), in1=free[:], op0=ALU.add,
                                         op1=ALU.mult).then_inc(s["fx_ok"], 1)
                wait(dve, s["fx_ok"], n)
                dve.tensor_tensor(blk_e[:], blk_e[:], fix[:], ALU.add).then_inc(s["be_ok"], 1)

            def weights(b, inverse_sums):
                n = b - 1
                for i in range(TB):
                    m = dve.max_index(top_i[:, i, :], top_s[:, i, :], score[:, i, :])
                m.then_inc(s["ti_ok"], 1)
                dve.reciprocal(top_w[:], top_s[:]).then_inc(s["pr_ok"], 1)
                wait(dve, s["ti_ok"], n)
                wait(dve, s["eo_ok"], n)
                shape = [P, TB, TOPK, TOPK]
                dve.tensor_tensor(eq[:], e_of[:].unsqueeze(3).broadcast_to(shape),
                                  top_i[:].unsqueeze(2).broadcast_to(shape), ALU.is_equal).then_inc(s["eq_ok"], 1)
                wait(dve, s["pr_ok"], n)
                dve.tensor_reduce(wsum[:], top_w[:], AX.X, ALU.add).then_inc(s["wc_ok"], 1)
                wait(dve, s["eq_ok"], n)
                dve.tensor_tensor(eqw[:], eq[:], top_w[:].unsqueeze(2).broadcast_to(shape), ALU.mult).then_inc(s["eqw_ok"], 1)
                inverse_sums()
                wait(dve, s["wc_ok"], n)
                dve.tensor_scalar(wsc[:], wsum[:], -1e-9, 1.0 / ROUTED_SCALE, ALU.add, ALU.mult).then_inc(s["wi_ok"], 1)
                wait(dve, s["eqw_ok"], n)
                dve.tensor_reduce(w_e[:], eqw[:], AX.X, ALU.add).then_inc(s["we_ok"], 1)
                wait(dve, s["wi_ok"], n)
                dve.reciprocal(winv[:], wsc[:]).then_inc(s["wn_ok"], 1)
                wait(dve, s["wn_ok"], n)
                wait(dve, s["we_ok"], n)
                dve.tensor_tensor(wE_res[:, bass.ds((b - 2) * TB, TB), :], w_e[:],
                                  winv[:].unsqueeze(2).broadcast_to([P, TB, TOPK]), ALU.mult).then_inc(s["wr_ok"], 1)

            def inverse_sums(b, g, step):
                if live(b, g, 1):
                    u = step - 1
                    wait(dve, s["p_ok"], 4 * u + 4)
                    wait(dve, s["pn_ok"], 3 * u - 3)
                    wait(dve, s["pna_ok"], u - 1)
                    dve.reciprocal(rinv[:, (g - 1) % 2], rowsum[:, (g - 1) % 2]).then_inc(s["ri_ok"], 1)

            def body(b):
                for g in range(G):
                    step = G * b + g
                    if live(b, g, 1):
                        u = step - 1
                        wait(dve, s["p_ok"], 4 * u - 4)
                        for h in range(2):
                            wait(dve, s["s_ps"], 2 * u + h + 1)
                            dve.tensor_reduce(negmax[:, (g - 1) % 2, h, :], psS[:, h, :].rearrange("p (i k) -> p i k", i=TB),
                                              AX.X, ALU.max, negate=True).then_inc(s["nm_ok"], 1)
                    if live(b, g, 0):
                        wait(dve, s["yh_ok"], step + 1)
                        wait(dve, s["s_ps"], 2 * (step - 1))
                        dve.tensor_tensor(y_lo[:, g % 2].rearrange("p a t -> p (a t)"), psY[:, 0, :],
                                          y_hi[:, g % 2].rearrange("p a t -> p (a t)").bitcast(F32), ALU.subtract).then_inc(s["yl_ok"], 1)
                    if g == 7 and live(b, g, 0):
                        input_split(b + 1)
                    if live(b, g, 3):
                        u = step - 3
                        wait(dve, s["o_ps"], u + 1)
                        wait(dve, s["ao_ps"], u - 1)
                        dve.tensor_copy(oT_sb[:, (g - 3) % 2, :], psO[:, 0, 0:SEQ]).then_inc(s["ot_ok"], 1)
                    if g == 7 or not seq(b, 2):
                        inverse_sums(b, g, step)
                    if seq(b, 2):
                        if g < 7:
                            (choose, slots, offsets, slot_numbers, new_state, chosen_slots, weights)[g](
                                b, lambda: inverse_sums(b, g, step))
                        else:
                            blocks(b)
                    if seq(b, 1):
                        if g == 3:
                            wait(dve, s["ao_ps"], G * b)
                            wait(dve, s["xb_ok"], b)
                            xr = x_res[:, bass.ds((b - 1) * TB, TB), :]
                            dve.tensor_tensor(xr, psA[:, 0, 0:SEQ].rearrange("p (i d) -> p i d", i=TB), xr, ALU.add).then_inc(s["x1_ok"], 1)
                            ln_stats(b - 1, "ln2", st2, mv2, ve2)
                        if g == 4:
                            wait(dve, s["x2t_ps"], b - 1)
                            wait(dve, s["xs_ok"], b - 1)
                            ln_apply(b - 1, "ln2", xn2, mv2, rs2)
                        if g == 5:
                            wait(dve, s["x2t_ps"], b)
                            wait(dve, s["lg_ps"], b - 1)
                            wait(dve, s["x2r_ok"], b - 1)
                            dve.tensor_copy(xn2T[:], psVM[:, 0, 0:SEQ]).then_inc(s["x2t_ok"], 1)
                        if g == 6:
                            wait(dve, s["lg_ps"], b)
                            wait(dve, s["ez_ok"], b - 1)
                            dve.tensor_tensor(z_sb[:], psVM[:, 0, 0:TB * E].rearrange("p (i e) -> p i e", i=TB), eb_sb[:], ALU.add).then_inc(s["z_ok"], 1)
                    if g == 4 and live(b, g, 0):
                        ln_stats(b + 1, "ln1", st1, mv1, ve1)
                    if g == 5 and live(b, g, 0):
                        wait(dve, s["xt_ps"], b + 1)
                        ln_apply(b + 1, "ln1", xn1, mv1, rs1)

            sequences(dve, body)

            def shared(n, r):
                dve.wait_ge(s["sho_ps"], n + 1)
                xr = x_res[:, bass.ds(4 * n, 4), :]
                dve.tensor_tensor(xr, psT[:, r, :].rearrange("p (i d) -> p i d", i=4), xr, ALU.add).then_inc(s["shared_ok"], 1)

            with dve.Fori(0, NT // 8) as it:
                for r in range(2):
                    shared(2 * it + r, r)

            dve.wait_ge(s["b_ps"], 1)
            dve.wait_ge(s["scat"], 16 * NT * TOPK)
            dve.tensor_scalar(blk_i[:], psY[:, 0, 0:NBLK], float(E - 1), None, ALU.min).then_inc(s["tab_ok"], 1)
            dve.wait_ge(s["tab_ok"], 1)

            dve.wait_ge(s["we_in"], 16 * ((E - E_EARLY) // 10 + E_EARLY // 10))

            def weights_of(r, n, first):
                if not first:
                    dve.wait_ge(s["y_ps"], n - RING + 1)
                for i, e in enumerate(experts_of(dve, n)):
                    m = dve.tensor_copy(w_b[:, r, i, :], w_all[:, bass.ds(e, 1), :].rearrange("p o i -> p (o i)"))
                m.then_inc(s["w_cp"], 1)

            def combine(n, q, r):
                dve.wait_ge(gat[r], 16 * TOPK * (q + 1))
                w = wE_res[:, bass.ds(n, 1), :].rearrange("p o k -> p (o k)").unsqueeze(2).broadcast_to([P, TOPK, D])
                dve.tensor_tensor(yg[:, r], yg[:, r], w, ALU.mult).then_inc(s["yw_ok"], 1)
                dve.wait_ge(s["yw_ok"], n + 1)
                if not isinstance(q, int) or q > 0:
                    dve.wait_ge(sto[r], 16 * q)
                dve.tensor_reduce(acc[:, r, :], yg[:, r].rearrange("p k d -> p d k"), AX.X, ALU.add).then_inc(s["ys_ok"], 1)
                dve.wait_ge(s["ys_ok"], n + 1)
                dve.tensor_tensor(acc[:, r, :], acc[:, r, :], x_res[:, bass.ds(n, 1), :].rearrange("p o d -> p (o d)"),
                                  ALU.add).then_inc(s["acc_ok"], 1)

            def turn(it):
                for r in range(RING):
                    weights_of(r, RING * it + r, False)

            for r in range(RING):
                weights_of(r, r, True)
            with dve.Fori(1, COMBINE_FROM) as it:
                turn(it)
            for k in range(YR):
                turn(COMBINE_FROM + k)
                combine(k, 0, k)
            with dve.Fori(1, (TURNS - COMBINE_FROM) // YR) as q:
                for k in range(YR):
                    turn(YR * q + (COMBINE_FROM + k))
                    combine(YR * q + k, q, k)
            with dve.Fori((TURNS - COMBINE_FROM) // YR, NT // YR) as q:
                for k in range(YR):
                    combine(YR * q + k, q, k)


_OUTS = [((B, SEQ, D), "float32")]


def kernel(**inputs):
    import numpy as _np
    import concourse.bacc as _bacc
    from concourse import mybir as _mybir
    from concourse.bass_utils import run_bass_kernel_spmd as _run

    pre = {k.replace("L0_attn_", "").replace("L0_ffn_", ""): _np.asarray(v) for k, v in inputs.items()}
    given = {
        "x": pre["x"], "WqT": pre["Wq"].T, "WkT": pre["Wk"].T, "Wv": pre["Wv"], "Wo": pre["Wo"], "bo": pre["bo"],
        "rwT": pre["router_w"].T, "ebias": pre["expert_bias"],
        "wgd": _np.concatenate([pre["w_gate"].transpose(2, 0, 1),
                                _np.tile(pre["w_down"].transpose(2, 0, 1), (2, 1, 1))], axis=2),
        "wgsT": pre["w_gate_shared"].T, "wdsT": pre["w_down_shared"].T,
    }
    nc = _bacc.Bacc("TRN2", target_bir_lowering=False, num_devices=1)
    arrays, args = {}, []
    for name, a in given.items():
        a = _np.ascontiguousarray(a)
        arrays[f"in_{name}_dram"] = a
        args.append(nc.dram_tensor(f"in_{name}_dram", a.shape, _mybir.dt.from_np(a.dtype), kind="ExternalInput").ap())
    for i, (shape, dtype) in enumerate(_OUTS):
        dt = _mybir.dt.from_np(_np.dtype(dtype))
        args.append(nc.dram_tensor(f"out_{i}_dram", shape, dt, kind="ExternalOutput").ap())
    build(nc, *args)
    r = _run(nc, [arrays], core_ids=[0])
    return r.results[0]["out_0_dram"]
```
